# Optimizing a Trainium2 kernel written in Bass

```python
import numpy as np
import jax
import jax.numpy as jnp

def _softmax(x, axis=-1):
    return jax.nn.softmax(x, axis=axis)

def _gelu(x):
    return jax.nn.gelu(x, approximate=True)

def _silu(x):
    return jax.nn.silu(x)

def _sigmoid(x):
    return jax.nn.sigmoid(x)

def _layernorm(x, axis=-1, eps=1e-05):
    m = jnp.mean(x, axis=axis, keepdims=True)
    v = jnp.var(x, axis=axis, keepdims=True)
    return (x - m) / jnp.sqrt(v + eps)

def _scatter_add(tgt, idx, src, axis=0):
    return tgt.at[idx].add(src)

def _segment_sum(src, seg, n):
    return jax.ops.segment_sum(src, seg, n)
kernel_name = 'mk_seq_preln_d1_jaxref_r4_3fe075'

def setup_inputs(seed: int=0):
    np.random.seed(seed)
    _w = jnp.asarray

    def _L0_attn_setup():
        import math
        import jax, jax.numpy as jnp
        import numpy as np
        HIDDEN = 256
        NUM_HEADS = 16
        NUM_QUERIES = 2
        NUM_Q_HEADS = NUM_HEADS * NUM_QUERIES
        HEAD_DIM = 64
        Q_DIM = NUM_Q_HEADS * HEAD_DIM
        KV_DIM = NUM_HEADS * HEAD_DIM
        BATCH, SEQ = (4, 256)

        def _alibi_slopes(num_heads: int) -> np.ndarray:
            closest_pow2 = 2 ** int(math.floor(math.log2(num_heads)))
            base = 2.0 ** (-2.0 ** (-(math.log2(closest_pow2) - 3)))
            powers = np.arange(1, closest_pow2 + 1, dtype=np.float32)
            slopes = base ** powers
            if closest_pow2 != num_heads:
                extra_base = 2.0 ** (-2.0 ** (-(math.log2(2 * closest_pow2) - 3)))
                extra_powers = np.arange(1, 2 * (num_heads - closest_pow2) + 1, 2, dtype=np.float32)
                slopes = np.concatenate([slopes, extra_base ** extra_powers])
            return slopes[:num_heads].astype(np.float32)
        ALIBI_SLOPES = jnp.asarray(_alibi_slopes(NUM_Q_HEADS))
        key = jax.random.key(seed)
        k1, k2, k3 = jax.random.split(key, 3)
        inputs = jax.random.normal(k1, (BATCH, SEQ, HIDDEN), dtype=jnp.float32)
        W_qkv = jax.random.normal(k2, (HIDDEN, Q_DIM + 2 * KV_DIM), dtype=jnp.float32) * (1.0 / math.sqrt(HIDDEN))
        W_out = jax.random.normal(k3, (Q_DIM, HIDDEN), dtype=jnp.float32) * (1.0 / math.sqrt(Q_DIM))
        return {'inputs': inputs, 'W_qkv': W_qkv, 'W_out': W_out}
    _L0_attn_in = _L0_attn_setup()

    def _L0_ffn_setup():
        import jax, jax.numpy as jnp
        import numpy as np
        D_MODEL, D_FF, RANK = (256, 1024, 64)
        B, S = (4, 1024)
        key = jax.random.key(seed)
        ks = jax.random.split(key, 7)
        return {'x': jax.random.normal(ks[0], (B, S, D_MODEL), dtype=jnp.float32), 'U1': jax.random.normal(ks[1], (D_MODEL, RANK), dtype=jnp.float32) * 0.02, 'V1': jax.random.normal(ks[2], (RANK, D_FF), dtype=jnp.float32) * 0.02, 'b1': jnp.zeros((D_FF,), dtype=jnp.float32), 'U2': jax.random.normal(ks[3], (D_FF, RANK), dtype=jnp.float32) * 0.02, 'V2': jax.random.normal(ks[4], (RANK, D_MODEL), dtype=jnp.float32) * 0.02, 'b2': jnp.zeros((D_MODEL,), dtype=jnp.float32)}
    _L0_ffn_in = _L0_ffn_setup()
    _d = {'L0_attn_inputs': _L0_attn_in['inputs'], 'L0_attn_W_qkv': _L0_attn_in['W_qkv'], 'L0_attn_W_out': _L0_attn_in['W_out'], 'L0_ffn_U1': _L0_ffn_in['U1'], 'L0_ffn_V1': _L0_ffn_in['V1'], 'L0_ffn_b1': _L0_ffn_in['b1'], 'L0_ffn_U2': _L0_ffn_in['U2'], 'L0_ffn_V2': _L0_ffn_in['V2'], 'L0_ffn_b2': _L0_ffn_in['b2']}
    _x0 = _d['L0_attn_inputs']
    _d['L0_attn_inputs'] = jax.random.normal(jax.random.fold_in(jax.random.key(seed), 1), (16, 512, 256), dtype=_x0.dtype)
    del _x0
    return _d

def reference(L0_attn_inputs, L0_attn_W_qkv, L0_attn_W_out, L0_ffn_U1, L0_ffn_V1, L0_ffn_b1, L0_ffn_U2, L0_ffn_V2, L0_ffn_b2):

    def _L0_attn_ref(inputs, W_qkv, W_out):
        import math
        import jax, jax.numpy as jnp
        import numpy as np
        HIDDEN = 256
        NUM_HEADS = 16
        NUM_QUERIES = 2
        NUM_Q_HEADS = NUM_HEADS * NUM_QUERIES
        HEAD_DIM = 64
        Q_DIM = NUM_Q_HEADS * HEAD_DIM
        KV_DIM = NUM_HEADS * HEAD_DIM
        BATCH, SEQ = (4, 256)

        def _alibi_slopes(num_heads: int) -> np.ndarray:
            closest_pow2 = 2 ** int(math.floor(math.log2(num_heads)))
            base = 2.0 ** (-2.0 ** (-(math.log2(closest_pow2) - 3)))
            powers = np.arange(1, closest_pow2 + 1, dtype=np.float32)
            slopes = base ** powers
            if closest_pow2 != num_heads:
                extra_base = 2.0 ** (-2.0 ** (-(math.log2(2 * closest_pow2) - 3)))
                extra_powers = np.arange(1, 2 * (num_heads - closest_pow2) + 1, 2, dtype=np.float32)
                slopes = np.concatenate([slopes, extra_base ** extra_powers])
            return slopes[:num_heads].astype(np.float32)
        ALIBI_SLOPES = jnp.asarray(_alibi_slopes(NUM_Q_HEADS))
        B, S, _ = inputs.shape
        qkv = inputs @ W_qkv
        q = qkv[..., :Q_DIM].reshape(B, S, NUM_Q_HEADS, HEAD_DIM).transpose(0, 2, 1, 3)
        k = qkv[..., Q_DIM:Q_DIM + KV_DIM].reshape(B, S, NUM_HEADS, HEAD_DIM).transpose(0, 2, 1, 3)
        v = qkv[..., Q_DIM + KV_DIM:].reshape(B, S, NUM_HEADS, HEAD_DIM).transpose(0, 2, 1, 3)
        k = jnp.repeat(k, NUM_QUERIES, axis=1)
        v = jnp.repeat(v, NUM_QUERIES, axis=1)
        pos = jnp.arange(S)
        rel = (pos[None, :] - pos[:, None]).astype(jnp.float32)
        bias = ALIBI_SLOPES[:, None, None] * rel[None, :, :]
        scores = jnp.einsum('bhqd,bhkd->bhqk', q, k) / math.sqrt(HEAD_DIM)
        scores = scores + bias[None]
        causal = pos[:, None] >= pos[None, :]
        scores = jnp.where(causal[None, None], scores, -jnp.inf)
        attn = jax.nn.softmax(scores, axis=-1)
        out = jnp.einsum('bhqk,bhkd->bhqd', attn, v)
        out = out.transpose(0, 2, 1, 3).reshape(B, S, Q_DIM)
        return out @ W_out

    def _L0_ffn_ref(x, U1, V1, b1, U2, V2, b2):
        import jax, jax.numpy as jnp
        import numpy as np
        D_MODEL, D_FF, RANK = (256, 1024, 64)
        B, S = (4, 1024)
        P = jnp.einsum('bsd,dr->bsr', x, U1)
        H = jax.nn.gelu(jnp.einsum('bsr,rf->bsf', P, V1) + b1)
        Q = jnp.einsum('bsf,fr->bsr', H, U2)
        return jnp.einsum('bsr,rd->bsd', Q, V2) + b2
    x = L0_attn_inputs
    x = x + _L0_attn_ref(_layernorm(x, axis=-1), L0_attn_W_qkv, L0_attn_W_out)
    x = x + _L0_ffn_ref(_layernorm(x, axis=-1), L0_ffn_U1, L0_ffn_V1, L0_ffn_b1, L0_ffn_U2, L0_ffn_V2, L0_ffn_b2)
    return x

_drawn_inputs = setup_inputs


def setup_inputs(seed=0):
    import zlib

    import numpy as np

    out = dict(_drawn_inputs(seed))
    spreads = {'L0_ffn_b1': (0.0, 0.8), 'L0_ffn_b2': (0.0, 0.8)}
    factors = {'L0_ffn_U1': 8.0, 'L0_ffn_V1': 8.0, 'L0_ffn_U2': 8.0, 'L0_ffn_V2': 8.0}
    for name, (base, spread) in spreads.items():
        noise = np.random.default_rng([zlib.crc32(name.encode()), seed]).standard_normal(out[name].shape)
        drawn = base * np.exp(spread * noise) if base else spread * noise
        out[name] = jnp.asarray(drawn.astype(out[name].dtype))
    for name, factor in factors.items():
        out[name] = (out[name] * factor).astype(out[name].dtype)
    return out
```

```python
from contextlib import ExitStack

import concourse.bass as bass
from concourse import mybir

F32 = mybir.dt.float32
F16 = mybir.dt.float16
BF16 = mybir.dt.bfloat16
ALU = mybir.AluOpType
ACT = mybir.ActivationFunctionType

P = 128
D = 256
DC = D // P
S = 512
T = S // P
HD = 64
KV = 16
QD = 2 * KV * HD
KD = KV * HD
FF = 1024
FC = FF // P
RANK = 64
RING = 8
SEG = 5
AUG = 10
AUG0, MAX0 = 64, 96
ATT = 7
EPS = 1e-5
W_SCALE, WO_SCALE, FFN_SCALE = 16.0, 32.0, 8.0
Q_OUT = 1.0 / (W_SCALE * 8.0)
KV_OUT = 1.0 / W_SCALE

SCORE_BLOCKS = [[(0, 0, 0, 512)], [(1, 0, 0, 512)],
                [(0, 1, 0, 384), (0, 3, 384, 128)], [(1, 1, 0, 384), (1, 3, 384, 128)],
                [(0, 2, 0, 256), (1, 2, 256, 256)]]
P_AT = {(h, kt): (n, off) for n, blocks in enumerate(SCORE_BLOCKS) for h, kt, off, _ in blocks}
MAX_BLOCKS = [[(0, 3, 0)], [(0, 2, 0), (0, 0, 384)], [(0, 1, 0), (1, 1, 256)],
              [(1, 3, 0)], [(1, 2, 0), (1, 0, 384)]]
FFN_PAIRS = {(13, 1): 0, (13, 3): 1, (14, 0): 2, (14, 2): 3}
U2_PAIRS = {(13, 3): 0, (14, 0): 1, (14, 2): 2, (14, 4): 3}
Y_PAIRS = {(15, 1): 0, (15, 3): 1}

FIRST, MID, LAST = "first", "mid", "last"


def has_proj(mode):
    return mode != LAST


def in_stage(mode, s, lag):
    return s >= lag if mode == FIRST else s < lag if mode == LAST else True


def layer(nc, x, w_qkv, w_out, u1, v1, b1, u2, v2, b2, k_aug, q_aug, ident_d, ident_b_d, causal_d, out):
    B = x.shape[0]
    ctx = ExitStack()
    with ctx:
        def sb(name, shape, dt):
            return ctx.enter_context(nc.sbuf_tensor(name, shape, dt))

        def psum(name):
            return ctx.enter_context(nc.psum_tensor(name, [P, 512], F32))

        def sem(name):
            return ctx.enter_context(nc.semaphore(name))

        wqkv = [sb(f"wqkv_{p}", [P, DC, QD + 2 * KD], F16) for p in ("hi", "lo")]
        wo = [sb(f"wo_{p}", [P, KV, D], F16) for p in ("hi", "lo")]
        u1s = [sb(f"u1_{p}", [P, DC, RANK], F16) for p in ("hi", "lo")]
        v1s = [sb(f"v1_{p}", [P, FF], F16) for p in ("hi", "lo")]
        v2s = [sb(f"v2_{p}", [P, D], F16) for p in ("hi", "lo")]
        u2s = sb("u2_hi_lo", [P, FC, 2 * RANK], F16)
        b1c = sb("b1_cols", [P, FC], F32)
        b2b = sb("b2_rows", [P, D], F32)
        ident = sb("ident", [P, P], F32)
        ident_b = sb("ident_bf16", [P, P], BF16)
        causal = sb("causal", [P, S], BF16)
        nhalf = sb("nhalf", [P, T], F32)
        qa = sb("q_hi_lo", [P, RING, 2, S], F16)
        qb = sb("q_hi_aug", [P, RING, 2, S], F16)
        ka = sb("k_lo_hi", [P, RING, S], F16)
        kb = sb("k_hi_aug", [P, RING, S], F16)
        v_hi = sb("v_hi_one", [P, T, KV, HD + 1], F16)
        v_lo = sb("v_lo", [P, T, KV, HD], F16)
        p_f = sb("p_f32", [P, 3, 512], F32)
        p_hi = sb("p_hi", [P, 2, SEG, 512], F16)
        p_lo = sb("p_lo", [P, 2, SEG, 512], F16)
        o_f = sb("o_f32", [P, T, 2 * HD], F32)
        rden = sb("rden", [P, 2, T], F32)
        ot = [sb(f"o_t_{p}", [P, KV, S], F16) for p in ("hi", "lo")]
        mcol = sb("row_max", [P, T, 8], F32)
        mt = [sb(f"neg_max_t_{p}", [8, S], F16) for p in ("hi", "lo")]
        xt = sb("x_rows", [P, T, D], F32)
        xnt = [sb(f"xn_t_{p}", [P, DC, S], F16) for p in ("hi", "lo")]
        bst = sb("bn_stats", [P, T, 6], F32)
        agg = sb("bn_aggr", [P, T, 2], F32)
        veps = sb("var_eps", [P, T], F32)
        rstd = sb("rstd", [P, T], F32)
        x2 = sb("x2_rows", [P, T, D], F32)
        bst2 = sb("bn_stats2", [P, T, 6], F32)
        agg2 = sb("bn_aggr2", [P, T, 2], F32)
        veps2 = sb("var_eps2", [P, T], F32)
        rstd2 = sb("rstd2", [P, T], F32)
        x2nt = [sb(f"x2n_t_{p}", [P, DC, P], F16) for p in ("hi", "lo")]
        pp = sb("ffn_p_hi_lo", [P, S], F16)
        h_f = sb("h_f32", [P, 2, S], F32)
        x2n = h_f[:, 0, 0:D]
        h_hi = sb("h_hi", [P, 2, S], F16)
        h_lo = sb("h_lo", [P, 2, S], F16)
        qf_hi, qf_lo = h_hi[:, 0, :], h_lo[:, 0, :]

        score_bank = [psum("scores0"), psum("scores1")]
        max_bank = psum("max_scores")
        o_bank = psum("o_acc")
        proj_bank = [psum("proj0"), psum("proj1")]
        t_bank = psum("transposes")
        ffn_bank = psum("ffn_acc")

        w_in = [sem(f"w_in{n}") for n in range(4)]
        const_in, split_hi, split_done, set_done = sem("const_in"), sem("split_hi"), sem("split_done"), sem("set_done")
        zeroed, qaug_in, x_in, k_rows = sem("zeroed"), sem("qaug_in"), sem("x_in"), sem("k_rows_set")
        x2_in, y_out = sem("x2_in"), sem("y_out")
        qdup_in = [sem(f"qdup_in{r}") for r in range(RING)]
        kdup_in = [sem(f"kdup_in{r}") for r in range(RING // 2)]
        kaug_in = [sem(f"kaug_in{r}") for r in range(RING // 2)]
        m_in = [sem("m_in0"), sem("m_in1")]
        pe_scores, pe_max, pe_av, pe_ot, pe_m = sem("pe_scores"), sem("pe_max"), sem("pe_av"), sem("pe_ot"), sem("pe_m")
        pe_ln1, pe_ln2, pe_q, pe_k, pe_v = sem("pe_ln1"), sem("pe_ln2"), sem("pe_q"), sem("pe_k"), sem("pe_v")
        pe_op, pe_pp, pe_h, pe_u2, pe_y = sem("pe_op"), sem("pe_pp"), sem("pe_h"), sem("pe_u2"), sem("pe_y")
        hi_q, hi_k, hi_v, hi_ot, hi_m = sem("hi_q"), sem("hi_k"), sem("hi_v"), sem("hi_ot"), sem("hi_m")
        hi_ln1, hi_ln2, hi_pp, hi_qf = sem("hi_ln1"), sem("hi_ln2"), sem("hi_pp"), sem("hi_qf")
        exp_done, hi_p, lo_p = sem("exp_done"), sem("hi_p"), sem("lo_p")
        gelu_done, hi_h, lo_h = sem("gelu_done"), sem("hi_h"), sem("lo_h")
        max_done, lo_q, lo_k, lo_v, lo_ot, lo_m = sem("max_done"), sem("lo_q"), sem("lo_k"), sem("lo_v"), sem("lo_ot"), sem("lo_m")
        lo_ln1, lo_ln2, lo_pp, lo_qf = sem("lo_ln1"), sem("lo_ln2"), sem("lo_pp"), sem("lo_qf")
        recip_done, o_done, y_done, b2_done = sem("recip_done"), sem("o_done"), sem("y_done"), sem("b2_done")
        st1, ag1, ve1, rs1, xn_done = sem("ln1_stats"), sem("ln1_aggr"), sem("ln1_veps"), sem("ln1_rstd"), sem("ln1_done")
        x2_done, st2, ag2, ve2, rs2, x2n_done = sem("x2_done"), sem("ln2_stats"), sem("ln2_aggr"), sem("ln2_veps"), sem("ln2_rstd"), sem("ln2_done")

        gate = sem("gate")

        block = ctx.enter_context(nc.Block())

        def wait(eng, semaphore, value):
            if not isinstance(value, int) or value > 0:
                eng.wait_ge(semaphore, value)

        def iterations(eng, body):
            body(0, FIRST)
            with eng.Fori(1, B) as i:
                body(i, MID)
            body(B, LAST)

        def x_src(b):
            return x[b].rearrange("(t p) d -> p t d", p=P)

        @block.sync
        def _(sp):
            stage = [qa, qb]
            for c in range(DC):
                sp.dma_start(stage[c][:, :, :, :].rearrange("p a b c -> p (a b c)").bitcast(F32),
                             w_qkv[c * P:(c + 1) * P, :]).then_inc(w_in[c], 16)
            sp.dma_start(xt[:, :, :], x_src(0)).then_inc(x_in, 16)
            sp.dma_start(ot[0][:, :, :].rearrange("p a b -> p (a b)").bitcast(F32).rearrange("p (c n) -> p c n", n=D),
                         w_out.rearrange("(c p) n -> p c n", p=P)).then_inc(w_in[2], 16)
            small = ot[1][:, :, :].rearrange("p a b -> p (a b)").bitcast(F32)
            for r in range(2):
                rows = slice(r * RANK, (r + 1) * RANK)
                sp.dma_start(small[rows, 0:FF], v1).then_inc(w_in[3], 16)
                sp.dma_start(small[rows, 1536:1536 + D], v2).then_inc(w_in[3], 16)
            sp.dma_start(small[:, 1024:1536].rearrange("p (c r) -> p c r", r=RANK),
                         u2.rearrange("(c p) r -> p c r", p=P)).then_inc(w_in[3], 16)
            sp.dma_start(small[:, 1792:1792 + DC * RANK].rearrange("p (c r) -> p c r", r=RANK),
                         u1.rearrange("(c p) r -> p c r", p=P)).then_inc(w_in[3], 16)
            sp.dma_start(ident[:, :], ident_d).then_inc(const_in, 16)
            sp.dma_start(causal[:, :], causal_d).then_inc(const_in, 16)
            sp.dma_start(ident_b[:, :], ident_b_d).then_inc(const_in, 16)
            sp.dma_start(b1c[:, :], b1).then_inc(const_in, 16)
            sp.dma_start(b2b[:, :], b2.rearrange("(o d) -> o d", o=1).to_broadcast([P, D])).then_inc(const_in, 16)
            sp.wait_ge(zeroed, 1)
            sp.wait_ge(k_rows, 2)
            sp.dma_start(qb[AUG0:AUG0 + AUG, :, :, :].rearrange("p a b c -> p (a b c)"), q_aug).then_inc(qaug_in, 16)

            def body(i, mode):
                for s in range(KV):
                    g = i * KV + s
                    if s % 4 == 2 and in_stage(mode, s, 6):
                        gr = i * 4 + (s - 6) // 4
                        sp.wait_ge(lo_m, gr + 1)
                        r0 = (s - 6) % RING
                        for part in range(2):
                            sp.dma_start(qb[MAX0 + part:MAX0 + part + 1, r0:r0 + 4, :, :].rearrange("o a b q -> o (a b) q"),
                                         mt[part][:, :]).then_inc(m_in[(s - 6) // 4 % 2], 16)
                    if mode != LAST:
                        if s % 2 == 1:
                            r0 = (s - 1) % RING
                            wait(sp, pe_scores, SEG * (i * KV + s - 7))
                            sp.dma_start(kb[AUG0:AUG0 + AUG, r0:r0 + 2, :],
                                         k_aug[:, s - 1:s + 1, :]).then_inc(kaug_in[r0 // 2], 16)
                            sp.wait_ge(hi_k, i * (KV // 2) + (s + 1) // 2)
                            sp.dma_start(ka[HD:P, r0:r0 + 2, :], kb[0:HD, r0:r0 + 2, :]).then_inc(kdup_in[r0 // 2], 16)
                        sp.wait_ge(hi_q, g + 1)
                        r = s % RING
                        sp.dma_start(qa[0:HD, r, :, :], qb[0:HD, r, :, :]).then_inc(qdup_in[r], 16)
                    if s == 2 and mode != FIRST:
                        wait(sp, y_out, 16 * (i - 1))
                        sp.dma_start(x2[:, :, :], x_src(i - 1)).then_inc(x2_in, 16)
                    if s == 4 and mode != LAST:
                        sp.wait_ge(pe_ln1, 2 * (i + 1))
                        sp.dma_start(xt[:, :, :], x_src((i + 1) % B)).then_inc(x_in, 16)
                if mode != FIRST:
                    sp.wait_ge(y_done, 2 * i)
                    sp.dma_start(out[i - 1].rearrange("(t p) d -> p t d", p=P), x2[:, :, :]).then_inc(y_out, 16)

            iterations(sp, body)
            sp.wait_ge(y_out, 16 * B)
            sp.wait_ge(x_in, 16 * (B + 1))

        @block.tensor
        def _(pe):
            def mm(out_ap, lhs, rhs, start, stop):
                return nc.tensor.matmul(out_ap, lhs, rhs, start=start, stop=stop, skip_group_check=True)

            def split_mm(out_ap, lhs, rhs, first=True, last=True):
                mm(out_ap, lhs[1], rhs[0], first, False)
                mm(out_ap, lhs[0], rhs[1], False, False)
                return mm(out_ap, lhs[0], rhs[0], False, last)

            pe.wait_ge(set_done, 1)
            pe.wait_ge(const_in, 80)
            pe.wait_ge(qaug_in, 16)
            pe.wait_ge(k_rows, 2)

            def body(i, mode):
                proj_free = [(lo_k, i * (KV // 2)), (lo_q, i * KV)]
                t_free = [(lo_ot, i * KV - 9)]
                turn = [0]

                def next_proj(semaphore, count):
                    b = turn[0] % 2
                    turn[0] += 1
                    wait(pe, *proj_free[b])
                    proj_free[b] = (semaphore, count)
                    return proj_bank[b]

                def transposes_bank(semaphore, count):
                    wait(pe, *t_free[0])
                    t_free[0] = (semaphore, count)
                    return t_bank

                def scores(s, n):
                    a = i * KV + s - ATT
                    r = (s - ATT) % RING
                    if n == 0:
                        use = 2 * i + (s - ATT) // RING + 1
                        pe.wait_ge(qdup_in[r], 16 * use)
                        pe.wait_ge(lo_q, a + 1)
                        if (s - ATT) % 2 == 0:
                            pe.wait_ge(kdup_in[r // 2], 16 * use)
                            pe.wait_ge(lo_k, i * (KV // 2) + (s - ATT) // 2 + 1)
                        if (s - ATT) % 4 == 0:
                            q4 = (s - ATT) // 4
                            pe.wait_ge(m_in[q4 % 2], 32 * (2 * i + q4 // 2 + 1))
                    wait(pe, exp_done, SEG * a + n - 1)
                    bank = score_bank[(SEG * s + n) % 2]
                    for h, kt, off, width in SCORE_BLOCKS[n]:
                        keys = slice(kt * P, (kt + 1) * P)
                        o = bank[:, off:off + width]
                        mm(o, ka[:, r, keys], qa[:, r, h, kt * P:S], True, False)
                        mm(o[:, 0:P], causal[:, S - P:S], ident_b[:, :], False, False)
                        last = mm(o, kb[:, r, keys], qb[:, r, h, kt * P:S], False, True)
                    last.then_inc(pe_scores, 1)

                def max_scores(s, n):
                    g = i * KV + s - 2
                    r = (s - 2) % RING
                    if n == 0:
                        pe.wait_ge(hi_q, g + 1)
                        if s % 2 == 0:
                            pe.wait_ge(hi_k, i * (KV // 2) + (s - 2) // 2 + 1)
                            pe.wait_ge(kaug_in[r // 2], 16 * (2 * i + (s - 2) // RING + 1))
                    wait(pe, max_done, SEG * g + n)
                    for h, qt, off in MAX_BLOCKS[n]:
                        width = (qt + 1) * P
                        last = mm(max_bank[:, off:off + width], qb[0:MAX0, r, h, qt * P:(qt + 1) * P],
                                  kb[0:MAX0, r, 0:width], True, True)
                    last.then_inc(pe_max, 1)

                def transpose_max(s):
                    gr = i * 4 + (s - 6) // 4
                    bank = transposes_bank(lo_m, gr + 1)
                    pe.wait_ge(max_done, 4 * SEG * (gr + 1))
                    for qt in range(T):
                        last = nc.tensor.transpose(bank[0:8, qt * P:(qt + 1) * P], mcol[:, qt, :], ident[:, :])
                    last.then_inc(pe_m, 1)

                def attend(s, h):
                    a = i * KV + s - ATT - 1
                    kv, slot = (s - ATT - 1) % KV, (s - 1) % 2
                    if h == 0:
                        pe.wait_ge(lo_p, SEG * (a + 1))
                        if kv % 8 == 0:
                            pe.wait_ge(lo_v, i * 8 + (4 if kv == 0 else 0))
                    wait(pe, o_done, 2 * a + h)
                    first = True
                    for qt in range(T):
                        for kt in range(qt + 1):
                            n, off = P_AT[h, kt]
                            cols = slice(off + (qt - kt) * P, off + (qt - kt + 1) * P)
                            o = o_bank[:, qt * (HD + 1):(qt + 1) * (HD + 1)]
                            mm(o, p_lo[:, slot, n, cols], v_hi[:, kt, kv, :], kt == 0, False)
                            mm(o[:, 0:HD], p_hi[:, slot, n, cols], v_lo[:, kt, kv, :], False, False)
                            last = mm(o, p_hi[:, slot, n, cols], v_hi[:, kt, kv, :], False, kt == qt)
                    last.then_inc(pe_av, 1)

                def transpose_o(s):
                    a = i * KV + s - ATT - 2
                    bank = transposes_bank(lo_ot, a + 1)
                    pe.wait_ge(o_done, 2 * (a + 1))
                    for qt in range(T):
                        last = nc.tensor.transpose(bank[:, qt * P:(qt + 1) * P], o_f[:, qt, :], ident[:, :])
                    last.then_inc(pe_ot, 1)

                def transpose_x(pair):
                    bank = transposes_bank(lo_ln1, i * 2 + pair + 1)
                    if pair == 0:
                        pe.wait_ge(xn_done, i + 1)
                    for c in range(DC):
                        for t in range(2):
                            col = (c * 2 + t) * P
                            last = nc.tensor.transpose(bank[:, col:col + P], xt[:, 2 * pair + t, c * P:(c + 1) * P], ident[:, :])
                    last.then_inc(pe_ln1, 1)

                def project(bank, col, semaphore):
                    for c in range(DC):
                        last = split_mm(bank[:, :], [w[:, c, col:col + P] for w in wqkv],
                                        [v[:, c, :] for v in xnt], c == 0, c == DC - 1)
                    last.then_inc(semaphore, 1)

                def project_v(s):
                    t, half = s % 8, s // 8
                    bank = next_proj(lo_v, i * 8 + half * 4 + t + 1)
                    col = QD + KD + half * 512
                    for c in range(DC):
                        last = split_mm(bank[:, :], [v[:, c, t * P:(t + 1) * P] for v in xnt],
                                        [w[:, c, col:col + 512] for w in wqkv], c == 0, c == DC - 1)
                    last.then_inc(pe_v, 1)

                def project_out(t):
                    bank = next_proj(x2_done, (i - 1) * 4 + t + 1)
                    if t == 0:
                        pe.wait_ge(lo_ot, i * KV)
                    for kv in range(KV):
                        last = split_mm(bank[:, 0:D], [o[:, kv, t * P:(t + 1) * P] for o in ot],
                                        [w[:, kv, :] for w in wo], kv == 0, kv == KV - 1)
                    last.then_inc(pe_op, 1)

                def transpose_x2(t):
                    u = (i - 1) * 4 + t
                    bank = transposes_bank(lo_ln2, u + 1)
                    pe.wait_ge(x2n_done, u + 1)
                    for c in range(DC):
                        last = nc.tensor.transpose(bank[:, c * P:(c + 1) * P], x2n[:, c * P:(c + 1) * P], ident[:, :])
                    last.then_inc(pe_ln2, 1)

                def ffn_p(t):
                    u = (i - 1) * 4 + t
                    bank = next_proj(lo_pp, u + 1)
                    pe.wait_ge(lo_ln2, u + 1)
                    for c in range(DC):
                        last = split_mm(bank[0:RANK, 0:P], [w[:, c, :] for w in u1s],
                                        [v[:, c, :] for v in x2nt], c == 0, c == DC - 1)
                    last.then_inc(pe_pp, 1)

                def ffn_h(pair):
                    for c in (2 * pair, 2 * pair + 1):
                        bank = next_proj(gelu_done, (i - 1) * FC + c + 1)
                        if c == 0:
                            pe.wait_ge(lo_pp, 4 * i)
                        mm(bank[:, :], v1s[1][:, c * P:(c + 1) * P], pp[:, :], True, False)
                        mm(bank[:, :], v1s[0][:, c * P:(c + 1) * P], pp[:, :], False, True).then_inc(pe_h, 1)

                def ffn_u2(pair):
                    for c in (2 * pair, 2 * pair + 1):
                        if c == 0:
                            wait(pe, y_done, 2 * (i - 1))
                        pe.wait_ge(lo_h, (i - 1) * FC + c + 1)
                        mm(ffn_bank[:, :], u2s[:, c, :], h_lo[:, c % 2, :], c == 0, False)
                        mm(ffn_bank[:, :], u2s[:, c, :], h_hi[:, c % 2, :], False, c == FC - 1).then_inc(pe_u2, 1)

                def ffn_y(pair):
                    if pair == 0:
                        pe.wait_ge(lo_qf, i)
                    else:
                        pe.wait_ge(y_done, 2 * i - 1)
                    for t in range(2):
                        tok = slice((2 * pair + t) * P, (2 * pair + t + 1) * P)
                        last = split_mm(ffn_bank[:, t * D:(t + 1) * D], [qf_hi[:, tok], qf_lo[:, tok]],
                                        [v[:, :] for v in v2s])
                    last.then_inc(pe_y, 1)

                for s in range(KV):
                    for n in range(SEG):
                        if in_stage(mode, s, ATT):
                            scores(s, n)
                        if n == 0 and s % 4 == 2 and in_stage(mode, s, 6):
                            transpose_max(s)
                        if in_stage(mode, s, 2):
                            max_scores(s, n)
                        if n == 0 and in_stage(mode, s, ATT + 2):
                            transpose_o(s)
                        if s == 0 and n < 2 and mode != LAST:
                            transpose_x(n)
                        if n == 0 and s % 2 == 1 and mode != LAST:
                            pair = (s - 1) // 2
                            project(next_proj(lo_k, i * (KV // 2) + pair + 1), QD + pair * P, pe_k)
                        if mode != FIRST:
                            if s == 8 and n >= 1:
                                project_out(n - 1)
                            if 9 <= s < 13 and n == 1:
                                transpose_x2(s - 9)
                            if (s, n) in U2_PAIRS:
                                ffn_u2(U2_PAIRS[s, n])
                            if (s, n) in FFN_PAIRS:
                                ffn_h(FFN_PAIRS[s, n])
                            if (s, n) in Y_PAIRS:
                                ffn_y(Y_PAIRS[s, n])
                        if n in (1, 3) and in_stage(mode, s, ATT + 1):
                            attend(s, n // 2)
                        if n == 3 and 9 <= s < 13 and mode != FIRST:
                            ffn_p(s - 9)
                        if n == 2 and mode != LAST:
                            if s == 0:
                                pe.wait_ge(lo_ln1, 2 * (i + 1))
                            project(next_proj(lo_q, i * KV + s + 1), s * P, pe_q)
                        if n == 4 and s % 8 < 4 and mode != LAST:
                            project_v(s)

            iterations(pe, body)

        @block.scalar
        def _(act):
            def copy(out_ap, in_ap, scale=1.0):
                return nc.scalar.activation(out_ap, in_ap, ACT.Copy, scale=scale)

            for c, stage in enumerate((qa, qb)):
                act.wait_ge(w_in[c], 16)
                src = stage[:, :, :, :].rearrange("p a b c -> p (a b c)").bitcast(F32)
                copy(wqkv[0][:, c, :], src, W_SCALE).then_inc(split_hi, 1)
            act.wait_ge(w_in[2], 16)
            copy(wo[0][:, :, :], ot[0][:, :, :].rearrange("p a b -> p (a b)").bitcast(F32).rearrange("p (c n) -> p c n", n=D),
                 WO_SCALE).then_inc(split_hi, 1)
            act.wait_ge(w_in[3], 96)
            small = ot[1][:, :, :].rearrange("p a b -> p (a b)").bitcast(F32)
            copy(v1s[0][:, :], small[:, 0:FF], FFN_SCALE)
            copy(u2s[:, :, 0:RANK], small[:, 1024:1536].rearrange("p (c r) -> p c r", r=RANK), FFN_SCALE)
            copy(v2s[0][:, :], small[:, 1536:1536 + D], FFN_SCALE)
            copy(u1s[0][:, :, :], small[:, 1792:1792 + DC * RANK].rearrange("p (c r) -> p c r", r=RANK),
                 FFN_SCALE).then_inc(split_hi, 1)
            act.wait_ge(const_in, 80)
            act.wait_ge(set_done, 1)

            def body(i, mode):
                turn = [0]

                def proj():
                    turn[0] += 1
                    return proj_bank[(turn[0] - 1) % 2]

                def exponentiate(s, n):
                    count = SEG * (i * KV + s - ATT) + n
                    act.wait_ge(pe_scores, count + 1)
                    back = 2 if s == 0 and n < 2 else 3
                    wait(act, lo_p, count - back + 1)
                    k = SEG * s + n
                    nc.scalar.activation(p_f[:, k % 3, :], score_bank[k % 2][:, :], ACT.Exp).then_inc(exp_done, 1)

                def high_p(s, n):
                    a = i * KV + s - ATT
                    act.wait_ge(exp_done, SEG * a + n + 1)
                    if n == 0:
                        wait(act, pe_av, 2 * (a - 1))
                    k = (SEG * s + n) % (SEG * KV)
                    copy(p_hi[:, s % 2, n, :], p_f[:, k % 3, :]).then_inc(hi_p, 1)

                for s in range(KV):
                    g = i * KV + s
                    for n in range(SEG):
                        if in_stage(mode, s, ATT):
                            exponentiate(s, n)
                        if n > 0 and in_stage(mode, s, ATT):
                            high_p(s, n - 1)
                        if n == 0 and in_stage(mode, s, ATT + 1):
                            if s > 0:
                                high_p(s - 1, SEG - 1)
                            else:
                                a = i * KV - ATT - 1
                                act.wait_ge(exp_done, SEG * (a + 1))
                                copy(p_hi[:, 1, SEG - 1, :], p_f[:, (SEG * KV - 1) % 3, :]).then_inc(hi_p, 1)
                        if n == 0 and s % 4 == 2 and in_stage(mode, s, 6):
                            gr = i * 4 + (s - 6) // 4
                            act.wait_ge(pe_m, gr + 1)
                            q4 = (s - 6) // 4 - 1
                            wait(act, m_in[q4 % 2], 32 * (2 * i + q4 // 2 + 1))
                            copy(mt[0][:, :], t_bank[0:8, :], -1.0).then_inc(hi_m, 1)
                        if n == 0 and in_stage(mode, s, ATT + 2):
                            a = g - ATT - 2
                            act.wait_ge(pe_ot, a + 1)
                            if s == ATT + 2:
                                wait(act, pe_op, 4 * i)
                            copy(ot[0][:, (s - ATT - 2) % KV, :], t_bank[:, :]).then_inc(hi_ot, 1)
                        if s == 0 and n < 2 and mode != LAST:
                            act.wait_ge(pe_ln1, i * 2 + n + 1)
                            if n == 0:
                                wait(act, pe_q, i * KV)
                            copy(xnt[0][:, :, n * 256:(n + 1) * 256],
                                 t_bank[:, :].rearrange("p (c q) -> p c q", c=DC)).then_inc(hi_ln1, 1)
                        if n == 0 and s % 2 == 1 and mode != LAST:
                            act.wait_ge(pe_k, i * (KV // 2) + (s + 1) // 2)
                            wait(act, pe_scores, SEG * (i * KV + s - 7))
                            bank, r0 = proj(), (s - 1) % RING
                            copy(kb[0:HD, r0, :], bank[0:HD, :], KV_OUT)
                            copy(kb[0:HD, r0 + 1, :], bank[HD:P, :], KV_OUT).then_inc(hi_k, 1)
                        if mode != FIRST:
                            if s == 8 and n >= 1:
                                proj()
                            if 9 <= s < 13 and n == 1:
                                u = (i - 1) * 4 + s - 9
                                act.wait_ge(pe_ln2, u + 1)
                                wait(act, pe_pp, u)
                                copy(x2nt[0][:, :, :], t_bank[:, 0:D].rearrange("p (c q) -> p c q", c=DC)).then_inc(hi_ln2, 1)
                            if (s, n) in FFN_PAIRS:
                                for c in (2 * FFN_PAIRS[s, n], 2 * FFN_PAIRS[s, n] + 1):
                                    act.wait_ge(pe_h, (i - 1) * FC + c + 1)
                                    wait(act, lo_h, (i - 1) * FC + max(c - 1, 0))
                                    nc.scalar.activation(h_f[:, c % 2, :], proj()[:, :], ACT.Gelu_apprx_tanh,
                                                         bias=b1c[:, c:c + 1], scale=1.0 / FFN_SCALE).then_inc(gelu_done, 1)
                            if (s, n) == (15, 0):
                                act.wait_ge(pe_u2, i * FC)
                                copy(qf_hi, ffn_bank[:, :], 1.0 / FFN_SCALE).then_inc(hi_qf, 1)
                        if n == 3 and 9 <= s < 13 and mode != FIRST:
                            u = (i - 1) * 4 + s - 9
                            act.wait_ge(pe_pp, u + 1)
                            if s == 9:
                                wait(act, pe_h, (i - 1) * FC)
                            copy(pp[0:RANK, (s - 9) * P:(s - 8) * P], proj()[0:RANK, 0:P], 1.0 / FFN_SCALE).then_inc(hi_pp, 1)
                        if n == 2 and mode != LAST:
                            act.wait_ge(pe_q, g + 1)
                            wait(act, pe_scores, SEG * (i * KV + s - 7))
                            bank, r = proj(), s % RING
                            copy(qb[0:HD, r, 0, :], bank[0:HD, :], Q_OUT)
                            copy(qb[0:HD, r, 1, :], bank[HD:P, :], Q_OUT).then_inc(hi_q, 1)
                        if n == 4 and s % 8 < 4 and mode != LAST:
                            t, half = s % 8, s // 8
                            act.wait_ge(pe_v, i * 8 + half * 4 + t + 1)
                            wait(act, pe_av, 2 * (i * KV + (0 if half else -8)))
                            copy(v_hi[:, t, half * 8:(half + 1) * 8, 0:HD],
                                 proj()[:, :].rearrange("p (k d) -> p k d", d=HD), KV_OUT).then_inc(hi_v, 1)

            iterations(act, body)

        @block.vector
        def _(dve):
            def low(out_ap, bank, high, scale):
                return nc.vector.scalar_tensor_tensor(out=out_ap, in0=bank, scalar=scale, in1=high,
                                                      op0=ALU.mult, op1=ALU.subtract)

            def ln1(b):
                dve.wait_ge(x_in, 16 * (b + 1))
                for t in range(T):
                    last = nc.vector.bn_stats(bst[:, t, :], xt[:, t, :])
                last.then_inc(st1, 1)
                dve.wait_ge(st1, b + 1)
                dve.sem_inc(gate, 1)
                for t in range(T):
                    last = nc.vector.bn_aggr(agg[:, t, :], bst[:, t, :])
                last.then_inc(ag1, 1)
                dve.wait_ge(ag1, b + 1)
                nc.vector.tensor_scalar(veps[:, :], agg[:, :, 1], EPS, None, ALU.add).then_inc(ve1, 1)
                dve.wait_ge(rs1, b + 1)
                for t in range(T):
                    last = nc.vector.tensor_scalar(xt[:, t, :], xt[:, t, :], agg[:, t, 0:1], rstd[:, t:t + 1],
                                                   ALU.subtract, ALU.mult)
                last.then_inc(xn_done, 1)

            nc.vector.memset(nhalf[:, :], -0.5).then_inc(split_done, 1)
            ln1(0)
            for c, stage in enumerate((qa, qb)):
                dve.wait_ge(split_hi, c + 1)
                src = stage[:, :, :, :].rearrange("p a b c -> p (a b c)").bitcast(F32)
                low(wqkv[1][:, c, :], src, wqkv[0][:, c, :], W_SCALE).then_inc(split_done, 1)
            dve.wait_ge(split_hi, 3)
            low(wo[1][:, :, :], ot[0][:, :, :].rearrange("p a b -> p (a b)").bitcast(F32).rearrange("p (c n) -> p c n", n=D),
                wo[0][:, :, :], WO_SCALE)
            dve.wait_ge(split_hi, 4)
            small = ot[1][:, :, :].rearrange("p a b -> p (a b)").bitcast(F32)
            low(v1s[1][:, :], small[:, 0:FF], v1s[0][:, :], FFN_SCALE)
            low(u2s[:, :, RANK:2 * RANK], small[:, 1024:1536].rearrange("p (c r) -> p c r", r=RANK),
                u2s[:, :, 0:RANK], FFN_SCALE)
            low(v2s[1][:, :], small[:, 1536:1536 + D], v2s[0][:, :], FFN_SCALE)
            low(u1s[1][:, :, :], small[:, 1792:1792 + DC * RANK].rearrange("p (c r) -> p c r", r=RANK),
                u1s[0][:, :, :], FFN_SCALE)
            nc.vector.memset(v_hi[:, :, :, HD:HD + 1], 1.0).then_inc(set_done, 1)
            dve.wait_ge(const_in, 80)

            def body(i, mode):
                turn = [0]

                def proj():
                    turn[0] += 1
                    return proj_bank[(turn[0] - 1) % 2]

                def maxima(s, n):
                    g = i * KV + s - 2
                    if n == 0 and (s - 2) % 4 == 0:
                        wait(dve, pe_m, i * 4 + (s - 2) // 4)
                    dve.wait_ge(pe_max, SEG * g + n + 1)
                    dve.sem_inc(gate, 1)
                    for h, qt, off in MAX_BLOCKS[n]:
                        bank = max_bank[:, off:off + (qt + 1) * P]
                        col = 2 * ((s - 2) % 4) + h
                        last = nc.vector.tensor_tensor_reduce(
                            out=bank, in0=bank, in1=causal[:, (T - 1 - qt) * P:S], scale=1.0, scalar=-3e38,
                            op0=ALU.add, op1=ALU.max, accum_out=mcol[:, qt, col:col + 1])
                    last.then_inc(max_done, 1)

                def normalise(s, h):
                    a = i * KV + s - ATT - 1
                    dve.wait_ge(pe_av, 2 * a + h + 1)
                    o = o_bank[:, 0:T * (HD + 1)].rearrange("p (t c) -> p t c", t=T)
                    nc.vector.reciprocal(rden[:, h, :], o[:, :, HD]).then_inc(recip_done, 1)
                    if h == 0:
                        wait(dve, pe_ot, a)
                    dve.wait_ge(recip_done, 2 * a + h + 1)
                    nc.vector.tensor_tensor(o_f[:, :, h * HD:(h + 1) * HD], o[:, :, 0:HD],
                                            rden[:, h, :].unsqueeze(2).to_broadcast([P, T, HD]),
                                            ALU.mult).then_inc(o_done, 1)

                for s in range(KV):
                    g = i * KV + s
                    for n in range(SEG):
                        if n == 0 and 9 <= s < 13 and mode != FIRST:
                            t = s - 9
                            u = (i - 1) * 4 + t
                            dve.wait_ge(rs2, u + 1)
                            if t == 0:
                                wait(dve, lo_h, (i - 1) * FC)
                            wait(dve, pe_ln2, u)
                            nc.vector.tensor_scalar(x2n[:, :], x2[:, t, :], agg2[:, t, 0:1], rstd2[:, t:t + 1],
                                                    ALU.subtract, ALU.mult).then_inc(x2n_done, 1)
                        if n == 0 and s % 4 == 2 and in_stage(mode, s, 6):
                            dve.wait_ge(hi_m, i * 4 + (s - 6) // 4 + 1)
                            low(mt[1][:, :], t_bank[0:8, :], mt[0][:, :], -1.0).then_inc(lo_m, 1)
                        if in_stage(mode, s, 2):
                            maxima(s, n)
                        if n == 0 and in_stage(mode, s, ATT + 2):
                            dve.wait_ge(hi_ot, g - ATT - 1)
                            low(ot[1][:, (s - ATT - 2) % KV, :], t_bank[:, :], ot[0][:, (s - ATT - 2) % KV, :],
                                1.0).then_inc(lo_ot, 1)
                        if s == 0 and n < 2 and mode != LAST:
                            dve.wait_ge(hi_ln1, i * 2 + n + 1)
                            cols = slice(n * 256, (n + 1) * 256)
                            low(xnt[1][:, :, cols], t_bank[:, :].rearrange("p (c q) -> p c q", c=DC),
                                xnt[0][:, :, cols], 1.0).then_inc(lo_ln1, 1)
                        if n == 0 and s % 2 == 1 and mode != LAST:
                            dve.wait_ge(hi_k, i * (KV // 2) + (s + 1) // 2)
                            bank, r0 = proj(), (s - 1) % RING
                            low(ka[0:HD, r0, :], bank[0:HD, :], kb[0:HD, r0, :], KV_OUT)
                            low(ka[0:HD, r0 + 1, :], bank[HD:P, :], kb[0:HD, r0 + 1, :], KV_OUT).then_inc(lo_k, 1)
                        if mode != FIRST:
                            if s == 8 and n >= 1:
                                t = n - 1
                                u = (i - 1) * 4 + t
                                if t == 0:
                                    dve.wait_ge(x2_in, 16 * i)
                                dve.wait_ge(pe_op, u + 1)
                                nc.vector.scalar_tensor_tensor(out=x2[:, t, :], in0=proj()[:, 0:D], scalar=1.0 / WO_SCALE,
                                                               in1=x2[:, t, :], op0=ALU.mult, op1=ALU.add).then_inc(x2_done, 1)
                                dve.wait_ge(x2_done, u + 1)
                                nc.vector.bn_stats(bst2[:, t, :], x2[:, t, :]).then_inc(st2, 1)
                                dve.wait_ge(st2, u + 1)
                                dve.sem_inc(gate, 1)
                                nc.vector.bn_aggr(agg2[:, t, :], bst2[:, t, :]).then_inc(ag2, 1)
                                dve.wait_ge(ag2, u + 1)
                                nc.vector.tensor_scalar(veps2[:, t:t + 1], agg2[:, t, 1:2], EPS, None, ALU.add).then_inc(ve2, 1)
                            if 9 <= s < 13 and n == 1:
                                u = (i - 1) * 4 + s - 9
                                dve.wait_ge(hi_ln2, u + 1)
                                low(x2nt[1][:, :, :], t_bank[:, 0:D].rearrange("p (c q) -> p c q", c=DC),
                                    x2nt[0][:, :, :], 1.0).then_inc(lo_ln2, 1)
                            if (s, n) in FFN_PAIRS:
                                for c in (2 * FFN_PAIRS[s, n], 2 * FFN_PAIRS[s, n] + 1):
                                    proj()
                                    dve.wait_ge(gelu_done, (i - 1) * FC + c + 1)
                                    if c >= 2:
                                        dve.wait_ge(pe_u2, (i - 1) * FC + c - 1)
                                    elif c == 0:
                                        wait(dve, pe_y, 2 * (i - 1))
                                    nc.vector.tensor_copy(h_hi[:, c % 2, :], h_f[:, c % 2, :]).then_inc(hi_h, 1)
                            if (s, n) == (15, 0):
                                dve.wait_ge(hi_qf, i)
                                low(qf_lo, ffn_bank[:, :], qf_hi, 1.0 / FFN_SCALE).then_inc(lo_qf, 1)
                            if (s, n) in Y_PAIRS:
                                pair = Y_PAIRS[s, n]
                                dve.wait_ge(pe_y, 2 * (i - 1) + pair + 1)
                                if pair == 0:
                                    dve.wait_ge(b2_done, 4 * i)
                                rows = x2[:, 2 * pair:2 * pair + 2, :]
                                nc.vector.scalar_tensor_tensor(out=rows, in0=ffn_bank[:, :].rearrange("p (t d) -> p t d", d=D),
                                                               scalar=1.0 / FFN_SCALE, in1=rows, op0=ALU.mult,
                                                               op1=ALU.add).then_inc(y_done, 1)
                        if n in (1, 3) and in_stage(mode, s, ATT + 1):
                            normalise(s, n // 2)
                        if n == 3 and 9 <= s < 13 and mode != FIRST:
                            dve.wait_ge(hi_pp, (i - 1) * 4 + s - 8)
                            cols = slice((s - 9) * P, (s - 8) * P)
                            low(pp[RANK:P, cols], proj()[0:RANK, 0:P], pp[0:RANK, cols], 1.0 / FFN_SCALE).then_inc(lo_pp, 1)
                        if n == 2 and mode != LAST:
                            dve.wait_ge(hi_q, g + 1)
                            bank, r = proj(), s % RING
                            low(qa[HD:P, r, 0, :], bank[0:HD, :], qb[0:HD, r, 0, :], Q_OUT)
                            low(qa[HD:P, r, 1, :], bank[HD:P, :], qb[0:HD, r, 1, :], Q_OUT).then_inc(lo_q, 1)
                        if n == 4 and s % 8 < 4 and mode != LAST:
                            t, half = s % 8, s // 8
                            heads = slice(half * 8, (half + 1) * 8)
                            dve.wait_ge(hi_v, i * 8 + half * 4 + t + 1)
                            low(v_lo[:, t, heads, :], proj()[:, :].rearrange("p (k d) -> p k d", d=HD),
                                v_hi[:, t, heads, 0:HD], KV_OUT).then_inc(lo_v, 1)
                    if s == 7 and mode != LAST:
                        ln1(i + 1)

            iterations(dve, body)

        @block.gpsimd
        def _(pool):
            pool.wait_ge(split_done, 1)

            def power1(b):
                pool.wait_ge(ve1, b + 1)
                nc.gpsimd.tensor_tensor(rstd[:, :], veps[:, :], nhalf[:, :], ALU.pow).then_inc(rs1, 1)

            power1(0)
            pool.wait_ge(rs1, 1)
            nc.gpsimd.memset(kb[HD:P, :, :], 0.0).then_inc(k_rows, 1)
            pool.wait_ge(k_rows, 1)
            nc.gpsimd.memset(kb[MAX0:MAX0 + 2, :, :], 1.0).then_inc(k_rows, 1)
            pool.wait_ge(k_rows, 2)
            pool.wait_ge(split_done, 3)
            nc.gpsimd.memset(qb[HD:P, :, :, :], 0.0).then_inc(zeroed, 1)
            pool.wait_ge(zeroed, 1)

            def body(i, mode):
                def low_p(count, slot, n, k):
                    pool.wait_ge(hi_p, count + 1)
                    nc.gpsimd.tensor_tensor(p_lo[:, slot, n, :], p_f[:, k % 3, :], p_hi[:, slot, n, :],
                                            ALU.subtract).then_inc(lo_p, 1)

                for s in range(KV):
                    for n in range(SEG):
                        if n > 0 and in_stage(mode, s, ATT):
                            low_p(SEG * (i * KV + s - ATT) + n - 1, s % 2, n - 1, SEG * s + n - 1)
                        if n == 0 and in_stage(mode, s, ATT + 1):
                            low_p(SEG * (i * KV + s - ATT) - 1, (s - 1) % 2, SEG - 1, (SEG * s - 1) % (SEG * KV))
                        if mode != FIRST:
                            if s == 8 and n >= 1:
                                t = n - 1
                                pool.wait_ge(ve2, (i - 1) * 4 + t + 1)
                                nc.gpsimd.tensor_tensor(rstd2[:, t:t + 1], veps2[:, t:t + 1], nhalf[:, 0:1],
                                                        ALU.pow).then_inc(rs2, 1)
                            if 9 <= s < 13 and n == 1:
                                t = s - 9
                                pool.wait_ge(x2n_done, (i - 1) * 4 + t + 1)
                                nc.gpsimd.tensor_tensor(x2[:, t, :], x2[:, t, :], b2b[:, :], ALU.add).then_inc(b2_done, 1)
                            if (s, n) in FFN_PAIRS:
                                for c in (2 * FFN_PAIRS[s, n], 2 * FFN_PAIRS[s, n] + 1):
                                    pool.wait_ge(hi_h, (i - 1) * FC + c + 1)
                                    nc.gpsimd.tensor_tensor(h_lo[:, c % 2, :], h_f[:, c % 2, :], h_hi[:, c % 2, :],
                                                            ALU.subtract).then_inc(lo_h, 1)
                    if s == 7 and mode != LAST:
                        power1(i + 1)

            pool.wait_ge(const_in, 80)
            iterations(pool, body)


_NAMES = ["L0_attn_inputs", "L0_attn_W_qkv", "L0_attn_W_out", "L0_ffn_U1", "L0_ffn_V1", "L0_ffn_b1",
          "L0_ffn_U2", "L0_ffn_V2", "L0_ffn_b2"]


def constants():
    import numpy as np

    slope = (np.float64(2.0) ** -0.25) ** np.arange(1, 2 * KV + 1)
    slope = slope.astype(np.float32).astype(np.float64)
    s1 = slope.astype(np.float16).astype(np.float64)
    s2 = (slope - s1).astype(np.float16).astype(np.float64)
    pos = np.arange(S, dtype=np.float64)
    sk = (s1 + s2)[:, None] * pos[None, :]
    parts = []
    for _ in range(3):
        part = sk.astype(np.float16).astype(np.float64)
        parts.append(part)
        sk = sk - part
    k_aug = np.zeros((AUG, KV, S), np.float16)
    q_aug = np.zeros((AUG, RING, 2, S), np.float16)
    for h in range(2):
        rows = [parts[0][h::2], np.broadcast_to(-s1[h::2, None], (KV, S)), parts[1][h::2],
                np.broadcast_to(-s2[h::2, None], (KV, S)), parts[2][h::2]]
        for j, row in enumerate(rows):
            k_aug[5 * h + j] = row.astype(np.float16)
            q_aug[5 * h + j, :, h, :] = (pos if j in (1, 3) else np.ones(S)).astype(np.float16)
    ident = np.eye(P, dtype=np.float32)
    causal = np.zeros((P, S), np.float32)
    causal[:, S - P:] = np.where(np.arange(P)[None, :] > np.arange(P)[:, None], np.float32(-1e30), np.float32(0))
    return k_aug, q_aug.reshape(AUG, RING * 2 * S), ident, causal


def kernel(**inputs):
    import ml_dtypes
    import numpy as _np
    import concourse.bacc as _bacc
    from concourse import mybir as _mybir
    from concourse.bass_utils import run_bass_kernel_spmd as _run

    nc = _bacc.Bacc("TRN2", target_bir_lowering=False, num_devices=1)
    arrays, args = {}, []
    k_aug, q_aug, ident, causal = constants()
    consts = {"k_aug": k_aug, "q_aug": q_aug, "ident": ident, "ident_b": ident.astype(ml_dtypes.bfloat16), "causal": causal.astype(ml_dtypes.bfloat16)}
    for name, a in [(n, inputs[n]) for n in _NAMES] + list(consts.items()):
        if name == "L0_ffn_b1":
            a = _np.asarray(a).reshape(FC, P).T
        a = _np.ascontiguousarray(a)
        arrays[f"in_{name}"] = a
        args.append(nc.dram_tensor(f"in_{name}", a.shape, _mybir.dt.from_np(a.dtype), kind="ExternalInput").ap())
    out = nc.dram_tensor("out_0", inputs["L0_attn_inputs"].shape, F32, kind="ExternalOutput").ap()
    layer(nc, *args, out)
    r = _run(nc, [arrays], core_ids=[0])
    return r.results[0]["out_0"]
```

```python
from contextlib import ExitStack

import concourse.bass as bass
from concourse import mybir

F32 = mybir.dt.float32
F16 = mybir.dt.float16
BF16 = mybir.dt.bfloat16
ALU = mybir.AluOpType
ACT = mybir.ActivationFunctionType

P = 128
D = 256
DC = D // P
S = 512
T = S // P
HD = 64
KV = 16
QD = 2 * KV * HD
KD = KV * HD
FF = 1024
FC = FF // P
RANK = 64
RING = 8
SEG = 5
AUG = 10
AUG0, MAX0 = 64, 96
ATT = 7
EPS = 1e-5
W_SCALE, WO_SCALE, FFN_SCALE = 16.0, 32.0, 8.0
Q_OUT = 1.0 / (W_SCALE * 8.0)
KV_OUT = 1.0 / W_SCALE

SCORE_BLOCKS = [[(0, 0, 0, 512)], [(1, 0, 0, 512)],
                [(0, 1, 0, 384), (0, 3, 384, 128)], [(1, 1, 0, 384), (1, 3, 384, 128)],
                [(0, 2, 0, 256), (1, 2, 256, 256)]]
P_AT = {(h, kt): (n, off) for n, blocks in enumerate(SCORE_BLOCKS) for h, kt, off, _ in blocks}
MAX_BLOCKS = [[(0, 3, 0)], [(0, 2, 0), (0, 0, 384)], [(0, 1, 0), (1, 1, 256)],
              [(1, 3, 0)], [(1, 2, 0), (1, 0, 384)]]
FFN_PAIRS = {(13, 1): 0, (13, 3): 1, (14, 0): 2, (14, 2): 3}
U2_PAIRS = {(13, 3): 0, (14, 0): 1, (14, 2): 2, (14, 4): 3}
Y_PAIRS = {(15, 2): 0, (15, 4): 1}
X_PAIRS = {(15, 3): 0, (15, 4): 1}


def out_segment(s):
    return 0 if 8 <= s < 13 else 1


MULTIPLES = (1, 2, 4, 8, 16, 32, 64, 80)

FREE = 1

FIRST, MID, LAST = "first", "mid", "last"


class Count:

    def __init__(self, i, regs=None, times=1, plus=0):
        self.i, self.regs, self.times, self.plus = i, regs, times, plus

    def __add__(self, n):
        return Count(self.i, self.regs, self.times, self.plus + n)

    __radd__ = __add__

    def __sub__(self, n):
        return self + -n

    def __mul__(self, n):
        return Count(self.i, self.regs, self.times * n, self.plus * n)

    __rmul__ = __mul__

    def __gt__(self, n):
        return bool(self.regs) or self.value() > n

    def value(self):
        return self.i * self.times + self.plus


def in_stage(mode, s, lag):
    return s >= lag if mode == FIRST else s < lag if mode == LAST else True


def layer(nc, x, w_qkv, w_out, u1, v1, b1, u2, v2, b2, k_aug, q_aug, ident_d, ident_b_d, causal_d, out):
    B = x.shape[0]
    ctx = ExitStack()
    with ctx:
        def sb(name, shape, dt):
            return ctx.enter_context(nc.sbuf_tensor(name, shape, dt))

        def psum(name):
            return ctx.enter_context(nc.psum_tensor(name, [P, 512], F32))

        def sem(name):
            return ctx.enter_context(nc.semaphore(name))

        wqkv = [sb(f"wqkv_{p}", [P, DC, QD + 2 * KD], F16) for p in ("hi", "lo")]
        wo = [sb(f"wo_{p}", [P, KV, D], F16) for p in ("hi", "lo")]
        u1s = [sb(f"u1_{p}", [P, DC, RANK], F16) for p in ("hi", "lo")]
        v1s = [sb(f"v1_{p}", [P, FF], F16) for p in ("hi", "lo")]
        v2s = [sb(f"v2_{p}", [P, D], F16) for p in ("hi", "lo")]
        u2s = sb("u2_hi_lo", [P, FC, 2 * RANK], F16)
        b1c = sb("b1_cols", [P, FC], F32)
        b2b = sb("b2_rows", [P, D], F32)
        ident = sb("ident", [P, P], F32)
        ident_b = sb("ident_bf16", [P, P], BF16)
        causal = sb("causal", [P, S], BF16)
        nhalf = sb("nhalf", [P, T], F32)
        qa = sb("q_hi_lo", [P, RING, 2, S], F16)
        qb = sb("q_hi_aug", [P, RING, 2, S], F16)
        ka = sb("k_lo_hi", [P, RING, S], F16)
        kb = sb("k_hi_aug", [P, RING, S], F16)
        v_hi = sb("v_hi_one", [P, T, KV, HD + 1], F16)
        v_lo = sb("v_lo", [P, T, KV, HD], F16)
        p_f = sb("p_f32", [P, 3, 512], F32)
        p_hi = sb("p_hi", [P, 2, SEG, 512], F16)
        p_lo = sb("p_lo", [P, 2, SEG, 512], F16)
        o_f = sb("o_f32", [P, T, 2 * HD], F32)
        rden = sb("rden", [P, 2, T], F32)
        ot = [sb(f"o_t_{p}", [P, KV, S], F16) for p in ("hi", "lo")]
        mcol = sb("row_max", [P, 2, T, 8], F32)
        mt = [sb(f"neg_max_t_{p}", [8, S], F16) for p in ("hi", "lo")]
        xt = sb("x_rows", [P, T, D], F32)
        xnt = [sb(f"xn_t_{p}", [P, DC, S], F16) for p in ("hi", "lo")]
        bst = sb("bn_stats", [P, T, 6], F32)
        agg = sb("bn_aggr", [P, T, 2], F32)
        veps = sb("var_eps", [P, T], F32)
        rstd = sb("rstd", [P, T], F32)
        x2 = sb("x2_rows", [P, T, D], F32)
        bst2 = sb("bn_stats2", [P, T, 6], F32)
        agg2 = sb("bn_aggr2", [P, T, 2], F32)
        veps2 = sb("var_eps2", [P, T], F32)
        rstd2 = sb("rstd2", [P, T], F32)
        x2nt = [sb(f"x2n_t_{p}", [P, DC, P], F16) for p in ("hi", "lo")]
        pp = sb("ffn_p_hi_lo", [P, S], F16)
        h_f = sb("h_f32", [P, 2, S], F32)
        x2n = h_f[:, 0, 0:D]
        h_hi = sb("h_hi", [P, 2, S], F16)
        h_lo = sb("h_lo", [P, 2, S], F16)
        qf_hi, qf_lo = h_hi[:, 0, :], h_lo[:, 0, :]

        score_bank = [psum("scores0"), psum("scores1")]
        max_bank = psum("max_scores")
        o_bank = psum("o_acc")
        proj_bank = [psum("proj0"), psum("proj1")]
        t_bank = psum("transposes")
        ffn_bank = psum("ffn_acc")

        w_in = [sem(f"w_in{n}") for n in range(4)]
        const_in, split_hi, split_done, set_done = sem("const_in"), sem("split_hi"), sem("split_done"), sem("set_done")
        zeroed, qaug_in, x_in, k_rows = sem("zeroed"), sem("qaug_in"), sem("x_in"), sem("k_rows_set")
        x2_in, y_out = sem("x2_in"), sem("y_out")
        qdup_in = [sem(f"qdup_in{r}") for r in range(RING)]
        kdup_in = [sem(f"kdup_in{r}") for r in range(RING // 2)]
        kaug_in = [sem(f"kaug_in{r}") for r in range(RING // 2)]
        m_in = [sem("m_in0"), sem("m_in1")]
        pe_scores, pe_max, pe_av, pe_ot, pe_m = sem("pe_scores"), sem("pe_max"), sem("pe_av"), sem("pe_ot"), sem("pe_m")
        pe_ln1, pe_ln2, pe_q, pe_k, pe_v = sem("pe_ln1"), sem("pe_ln2"), sem("pe_q"), sem("pe_k"), sem("pe_v")
        pe_op, pe_pp, pe_h, pe_u2, pe_y = sem("pe_op"), sem("pe_pp"), sem("pe_h"), sem("pe_u2"), sem("pe_y")
        hi_q, hi_k, hi_v, hi_ot, hi_m = sem("hi_q"), sem("hi_k"), sem("hi_v"), sem("hi_ot"), sem("hi_m")
        hi_ln1, hi_ln2, hi_pp, hi_qf = sem("hi_ln1"), sem("hi_ln2"), sem("hi_pp"), sem("hi_qf")
        exp_done, hi_p, lo_p = sem("exp_done"), sem("hi_p"), sem("lo_p")
        gelu_done, hi_h, lo_h = sem("gelu_done"), sem("hi_h"), sem("lo_h")
        max_done, lo_q, lo_k, lo_v, lo_ot, lo_m = sem("max_done"), sem("lo_q"), sem("lo_k"), sem("lo_v"), sem("lo_ot"), sem("lo_m")
        lo_ln1, lo_ln2, lo_pp, lo_qf = sem("lo_ln1"), sem("lo_ln2"), sem("lo_pp"), sem("lo_qf")
        recip_done, o_done, y_done, b2_done = sem("recip_done"), sem("o_done"), sem("y_done"), sem("b2_done")
        st1, ag1, ve1, rs1, xn_done = sem("ln1_stats"), sem("ln1_aggr"), sem("ln1_veps"), sem("ln1_rstd"), sem("ln1_done")
        x2_done, st2, ag2, ve2, rs2, x2n_done = sem("x2_done"), sem("ln2_stats"), sem("ln2_aggr"), sem("ln2_veps"), sem("ln2_rstd"), sem("ln2_done")

        gate = sem("gate")

        block = ctx.enter_context(nc.Block())

        def at(count):
            if not isinstance(count, Count):
                return count
            if not count.regs:
                return count.value()
            if not count.plus:
                return count.regs[count.times]
            count.regs["eng"].reg_add(count.regs["target"], count.regs[count.times], count.plus)
            return count.regs["target"]

        def max_place(s, n):
            k = SEG * s + n
            if s >= 13:
                return max_bank, 1
            back = 1 if k == 0 else 2
            return (ffn_bank if k % 2 else max_bank), back

        def iterations(name, eng, body):
            body(Count(0), FIRST)
            regs = {n: eng.alloc_register(f"{name}_{n}") for n in (*MULTIPLES, "target")}
            regs["eng"] = eng
            with eng.Fori(1, B) as i:
                for times in MULTIPLES:
                    eng.reg_mul(regs[times], i, times)
                body(Count(i, regs), MID)
            body(Count(B), LAST)

        def x_src(b):
            return x[b].rearrange("(t p) d -> p t d", p=P)

        @block.sync
        def _(sp):
            sp.sem_inc(y_out, FREE)
            stage = [qa, qb]
            for c in range(DC):
                sp.dma_start(stage[c][:, :, :, :].rearrange("p a b c -> p (a b c)").bitcast(F32),
                             w_qkv[c * P:(c + 1) * P, :]).then_inc(w_in[c], 16)
            sp.dma_start(xt[:, :, :], x_src(0)).then_inc(x_in, 16)
            sp.dma_start(ot[0][:, :, :].rearrange("p a b -> p (a b)").bitcast(F32).rearrange("p (c n) -> p c n", n=D),
                         w_out.rearrange("(c p) n -> p c n", p=P)).then_inc(w_in[2], 16)
            small = ot[1][:, :, :].rearrange("p a b -> p (a b)").bitcast(F32)
            for r in range(2):
                rows = slice(r * RANK, (r + 1) * RANK)
                sp.dma_start(small[rows, 0:FF], v1).then_inc(w_in[3], 16)
                sp.dma_start(small[rows, 1536:1536 + D], v2).then_inc(w_in[3], 16)
            sp.dma_start(small[:, 1024:1536].rearrange("p (c r) -> p c r", r=RANK),
                         u2.rearrange("(c p) r -> p c r", p=P)).then_inc(w_in[3], 16)
            sp.dma_start(small[:, 1792:1792 + DC * RANK].rearrange("p (c r) -> p c r", r=RANK),
                         u1.rearrange("(c p) r -> p c r", p=P)).then_inc(w_in[3], 16)
            sp.dma_start(ident[:, :], ident_d).then_inc(const_in, 16)
            sp.dma_start(causal[:, :], causal_d).then_inc(const_in, 16)
            sp.dma_start(ident_b[:, :], ident_b_d).then_inc(const_in, 16)
            sp.dma_start(b1c[:, :], b1).then_inc(const_in, 16)
            sp.dma_start(b2b[:, :], b2.rearrange("(o d) -> o d", o=1).to_broadcast([P, D])).then_inc(const_in, 16)
            sp.wait_ge(zeroed, 1)
            sp.wait_ge(k_rows, 2)
            sp.dma_start(qb[AUG0:AUG0 + AUG, :, :, :].rearrange("p a b c -> p (a b c)"), q_aug).then_inc(qaug_in, 16)

            def body(i, mode):
                for s in range(KV):
                    g = i * KV + s
                    if s % 4 == 2 and in_stage(mode, s, 6):
                        gr = i * 4 + (s - 6) // 4
                        sp.wait_ge(lo_m, at(gr + 1))
                        r0 = (s - 6) % RING
                        for part in range(2):
                            sp.dma_start(qb[MAX0 + part:MAX0 + part + 1, r0:r0 + 4, :, :].rearrange("o a b q -> o (a b) q"),
                                         mt[part][:, :]).then_inc(m_in[(s - 6) // 4 % 2], 16)
                    if mode != LAST:
                        if s % 2 == 1:
                            r0 = (s - 1) % RING
                            if SEG * (i * KV + s - 7) > 0:
                                sp.wait_ge(pe_scores, at(SEG * (i * KV + s - 7)))
                            sp.dma_start(kb[AUG0:AUG0 + AUG, r0:r0 + 2, :],
                                         k_aug[:, s - 1:s + 1, :]).then_inc(kaug_in[r0 // 2], 16)
                            sp.wait_ge(hi_k, at(i * (KV // 2) + (s + 1) // 2))
                            sp.dma_start(ka[HD:P, r0:r0 + 2, :], kb[0:HD, r0:r0 + 2, :]).then_inc(kdup_in[r0 // 2], 16)
                        sp.wait_ge(hi_q, at(g + 1))
                        r = s % RING
                        sp.dma_start(qa[0:HD, r, :, :], qb[0:HD, r, :, :]).then_inc(qdup_in[r], 16)
                    if s == 2 and mode != FIRST:
                        sp.wait_ge(y_out, at(16 * (i - 1) + FREE))
                        sp.dma_start(x2[:, :, :], x_src((i - 1).value())).then_inc(x2_in, 16)
                    if s == 4 and mode != LAST:
                        sp.wait_ge(pe_ln1, at(2 * (i + 1)))
                        sp.dma_start(xt[:, :, :], x_src((i + 1).value() % B)).then_inc(x_in, 16)
                if mode != FIRST:
                    sp.wait_ge(y_done, at(2 * i + FREE))
                    sp.dma_start(out[(i - 1).value()].rearrange("(t p) d -> p t d", p=P), x2[:, :, :]).then_inc(y_out, 16)

            iterations("sp", sp, body)
            sp.wait_ge(y_out, 16 * B + FREE)
            sp.wait_ge(x_in, 16 * (B + 1))

        @block.tensor
        def _(pe):
            pe.sem_inc(pe_pp, FREE)
            pe.sem_inc(pe_h, FREE)
            pe.sem_inc(pe_ln2, FREE)
            pe.sem_inc(pe_y, FREE)

            def mm(out_ap, lhs, rhs, start, stop):
                return nc.tensor.matmul(out_ap, lhs, rhs, start=start, stop=stop, skip_group_check=True)

            def split_mm(out_ap, lhs, rhs, first=True, last=True):
                mm(out_ap, lhs[1], rhs[0], first, False)
                mm(out_ap, lhs[0], rhs[1], False, False)
                return mm(out_ap, lhs[0], rhs[0], False, last)

            pe.wait_ge(set_done, 1)
            pe.wait_ge(const_in, 80)
            pe.wait_ge(qaug_in, 16)
            pe.wait_ge(k_rows, 2)

            def transpose_x(b, pair):
                if pair == 0:
                    pe.wait_ge(xn_done, at(b + 1))
                for c in range(DC):
                    for t in range(2):
                        col = (c * 2 + t) * P
                        last = nc.tensor.transpose(t_bank[:, col:col + P], xt[:, 2 * pair + t, c * P:(c + 1) * P], ident[:, :])
                last.then_inc(pe_ln1, 1)

            transpose_x(0, 0)
            pe.wait_ge(lo_ln1, 1)
            transpose_x(0, 1)

            def body(i, mode):
                proj_free = [(lo_k, i * (KV // 2)), (lo_q, i * KV)]
                t_free = [(lo_ln1, 2 * (i + 1))]
                turn = [0]

                def next_proj(semaphore, count):
                    b = turn[0] % 2
                    turn[0] += 1
                    read, times = proj_free[b]
                    if times > 0:
                        pe.wait_ge(read, at(times))
                    proj_free[b] = (semaphore, count)
                    return proj_bank[b]

                def transposes_bank(semaphore, count):
                    read, times = t_free[0]
                    if times > 0:
                        pe.wait_ge(read, at(times))
                    t_free[0] = (semaphore, count)
                    return t_bank

                def scores(s, n):
                    a = i * KV + s - ATT
                    r = (s - ATT) % RING
                    if n == 0:
                        use = 2 * i + (s - ATT) // RING + 1
                        pe.wait_ge(qdup_in[r], at(16 * use))
                        pe.wait_ge(lo_q, at(a + 1))
                        if (s - ATT) % 2 == 0:
                            pe.wait_ge(kdup_in[r // 2], at(16 * use))
                            pe.wait_ge(lo_k, at(i * (KV // 2) + (s - ATT) // 2 + 1))
                        if (s - ATT) % 4 == 0:
                            q4 = (s - ATT) // 4
                            pe.wait_ge(m_in[q4 % 2], at(32 * (2 * i + q4 // 2 + 1)))
                    if SEG * a + n - 1 > 0:
                        pe.wait_ge(exp_done, at(SEG * a + n - 1))
                    bank = score_bank[(SEG * s + n) % 2]
                    for h, kt, off, width in SCORE_BLOCKS[n]:
                        keys = slice(kt * P, (kt + 1) * P)
                        o = bank[:, off:off + width]
                        mm(o, ka[:, r, keys], qa[:, r, h, kt * P:S], True, False)
                        mm(o[:, 0:P], causal[:, S - P:S], ident_b[:, :], False, False)
                        last = mm(o, kb[:, r, keys], qb[:, r, h, kt * P:S], False, True)
                    last.then_inc(pe_scores, 1)

                def max_scores(s, n):
                    g = i * KV + s - 2
                    r = (s - 2) % RING
                    if n == 0:
                        pe.wait_ge(hi_q, at(g + 1))
                        if s % 2 == 0:
                            pe.wait_ge(hi_k, at(i * (KV // 2) + (s - 2) // 2 + 1))
                            pe.wait_ge(kaug_in[r // 2], at(16 * (2 * i + (s - 2) // RING + 1)))
                    bank, back = max_place(s, n)
                    if (s, n) == (0, 1) and mode != FIRST:
                        pe.wait_ge(y_done, at(2 * (i - 1) + FREE))
                    if SEG * g + n + 1 - back > 0:
                        pe.wait_ge(max_done, at(SEG * g + n + 1 - back))
                    for h, qt, off in MAX_BLOCKS[n]:
                        width = (qt + 1) * P
                        last = mm(bank[:, off:off + width], qb[0:MAX0, r, h, qt * P:(qt + 1) * P],
                                  kb[0:MAX0, r, 0:width], True, True)
                    last.then_inc(pe_max, 1)

                def transpose_max(s):
                    gr = i * 4 + (s - 6) // 4
                    bank = next_proj(lo_m, gr + 1)
                    pe.wait_ge(max_done, at(4 * SEG * (gr + 1)))
                    for qt in range(T):
                        last = nc.tensor.transpose(bank[0:8, qt * P:(qt + 1) * P], mcol[:, (s - 6) // 4 % 2, qt, :], ident[:, :])
                    last.then_inc(pe_m, 1)

                def attend(s, h):
                    a = i * KV + s - ATT - 1
                    kv, slot = (s - ATT - 1) % KV, (s - 1) % 2
                    if h == 0:
                        pe.wait_ge(lo_p, at(SEG * (a + 1)))
                        if kv % 8 == 0:
                            pe.wait_ge(lo_v, at(i * 8 + (4 if kv == 0 else 0)))
                    if 2 * a + h > 0:
                        pe.wait_ge(o_done, at(2 * a + h))
                    first = True
                    for qt in range(T):
                        for kt in range(qt + 1):
                            n, off = P_AT[h, kt]
                            cols = slice(off + (qt - kt) * P, off + (qt - kt + 1) * P)
                            o = o_bank[:, qt * (HD + 1):(qt + 1) * (HD + 1)]
                            mm(o, p_lo[:, slot, n, cols], v_hi[:, kt, kv, :], kt == 0, False)
                            mm(o[:, 0:HD], p_hi[:, slot, n, cols], v_lo[:, kt, kv, :], False, False)
                            last = mm(o, p_hi[:, slot, n, cols], v_hi[:, kt, kv, :], False, kt == qt)
                    last.then_inc(pe_av, 1)

                def transpose_o(s):
                    a = i * KV + s - ATT - 2
                    bank = transposes_bank(lo_ot, a + 1)
                    pe.wait_ge(o_done, at(2 * (a + 1)))
                    for qt in range(T):
                        last = nc.tensor.transpose(bank[:, qt * P:(qt + 1) * P], o_f[:, qt, :], ident[:, :])
                    last.then_inc(pe_ot, 1)

                def project(bank, col, semaphore):
                    for c in range(DC):
                        last = split_mm(bank[:, :], [w[:, c, col:col + P] for w in wqkv],
                                        [v[:, c, :] for v in xnt], c == 0, c == DC - 1)
                    last.then_inc(semaphore, 1)

                def project_v(s):
                    t, half = s % 8, s // 8
                    bank = next_proj(lo_v, i * 8 + half * 4 + t + 1)
                    col = QD + KD + half * 512
                    for c in range(DC):
                        last = split_mm(bank[:, :], [v[:, c, t * P:(t + 1) * P] for v in xnt],
                                        [w[:, c, col:col + 512] for w in wqkv], c == 0, c == DC - 1)
                    last.then_inc(pe_v, 1)

                def project_out(t):
                    bank = next_proj(x2_done, (i - 1) * 4 + t + 1)
                    for kv in range(KV):
                        if t == 0 and kv == KV - 1:
                            pe.wait_ge(lo_ot, at(i * KV))
                        last = split_mm(bank[:, 0:D], [o[:, kv, t * P:(t + 1) * P] for o in ot],
                                        [w[:, kv, :] for w in wo], kv == 0, kv == KV - 1)
                    last.then_inc(pe_op, 1)

                def transpose_x2(t):
                    u = (i - 1) * 4 + t
                    bank = transposes_bank(lo_ln2, u + 1)
                    pe.wait_ge(x2n_done, at(u + 1))
                    for c in range(DC):
                        last = nc.tensor.transpose(bank[:, c * P:(c + 1) * P], x2n[:, c * P:(c + 1) * P], ident[:, :])
                    last.then_inc(pe_ln2, 1)

                def ffn_p(t):
                    u = (i - 1) * 4 + t
                    bank = next_proj(lo_pp, u + 1)
                    pe.wait_ge(lo_ln2, at(u + 1))
                    for c in range(DC):
                        last = split_mm(bank[0:RANK, 0:P], [w[:, c, :] for w in u1s],
                                        [v[:, c, :] for v in x2nt], c == 0, c == DC - 1)
                    last.then_inc(pe_pp, 1)

                def ffn_h(pair):
                    for c in (2 * pair, 2 * pair + 1):
                        bank = next_proj(gelu_done, (i - 1) * FC + c + 1)
                        if c == 0:
                            pe.wait_ge(lo_pp, at(4 * i))
                        mm(bank[:, :], v1s[1][:, c * P:(c + 1) * P], pp[:, :], True, False)
                        mm(bank[:, :], v1s[0][:, c * P:(c + 1) * P], pp[:, :], False, True).then_inc(pe_h, 1)

                def ffn_u2(pair):
                    for c in (2 * pair, 2 * pair + 1):
                        if c == 0:
                            pe.wait_ge(y_done, at(2 * (i - 1) + FREE))
                        pe.wait_ge(lo_h, at((i - 1) * FC + c + 1 + FREE))
                        mm(ffn_bank[:, :], u2s[:, c, :], h_lo[:, c % 2, :], c == 0, False)
                        mm(ffn_bank[:, :], u2s[:, c, :], h_hi[:, c % 2, :], False, c == FC - 1).then_inc(pe_u2, 1)

                def ffn_y(pair):
                    if pair == 0:
                        pe.wait_ge(lo_qf, at(i))
                    else:
                        pe.wait_ge(y_done, at(2 * i - 1 + FREE))
                    for t in range(2):
                        tok = slice((2 * pair + t) * P, (2 * pair + t + 1) * P)
                        last = split_mm(ffn_bank[:, t * D:(t + 1) * D], [qf_hi[:, tok], qf_lo[:, tok]],
                                        [v[:, :] for v in v2s])
                    last.then_inc(pe_y, 1)

                for s in range(KV):
                    for n in range(SEG):
                        if in_stage(mode, s, ATT):
                            scores(s, n)
                        if n == 1 and s % 4 == 2 and in_stage(mode, s, 6):
                            transpose_max(s)
                        if in_stage(mode, s, 2):
                            max_scores(s, n)
                        if n == out_segment(s) and in_stage(mode, s, ATT + 2):
                            transpose_o(s)
                        if (s, n) in X_PAIRS and mode != LAST:
                            pair = X_PAIRS[s, n]
                            transposes_bank(lo_ln1, 2 * (i + 1) + pair + 1)
                            transpose_x(i + 1, pair)
                        if n == 0 and s % 2 == 1 and mode != LAST:
                            pair = (s - 1) // 2
                            project(next_proj(lo_k, i * (KV // 2) + pair + 1), QD + pair * P, pe_k)
                        if mode != FIRST:
                            if s == 8 and n >= 1:
                                project_out(n - 1)
                            if 9 <= s < 13 and n == 2:
                                transpose_x2(s - 9)
                            if (s, n) in U2_PAIRS:
                                ffn_u2(U2_PAIRS[s, n])
                            if (s, n) in FFN_PAIRS:
                                ffn_h(FFN_PAIRS[s, n])
                            if (s, n) in Y_PAIRS:
                                ffn_y(Y_PAIRS[s, n])
                        if n in (1, 3) and in_stage(mode, s, ATT + 1):
                            attend(s, n // 2)
                        if n == 2 and mode != LAST:
                            if s == 0:
                                pe.wait_ge(lo_ln1, at(2 * (i + 1)))
                            project(next_proj(lo_q, i * KV + s + 1), s * P, pe_q)
                        if n == 4 and s % 8 < 4 and mode != LAST:
                            project_v(s)
                        if n == 4 and 9 <= s < 13 and mode != FIRST:
                            ffn_p(s - 9)

            iterations("pe", pe, body)

        @block.scalar
        def _(act):
            def copy(out_ap, in_ap, scale=1.0):
                return nc.scalar.activation(out_ap, in_ap, ACT.Copy, scale=scale)

            for c, stage in enumerate((qa, qb)):
                act.wait_ge(w_in[c], 16)
                src = stage[:, :, :, :].rearrange("p a b c -> p (a b c)").bitcast(F32)
                copy(wqkv[0][:, c, :], src, W_SCALE).then_inc(split_hi, 1)
            act.wait_ge(w_in[2], 16)
            copy(wo[0][:, :, :], ot[0][:, :, :].rearrange("p a b -> p (a b)").bitcast(F32).rearrange("p (c n) -> p c n", n=D),
                 WO_SCALE).then_inc(split_hi, 1)
            act.wait_ge(w_in[3], 96)
            small = ot[1][:, :, :].rearrange("p a b -> p (a b)").bitcast(F32)
            copy(v1s[0][:, :], small[:, 0:FF], FFN_SCALE)
            copy(u2s[:, :, 0:RANK], small[:, 1024:1536].rearrange("p (c r) -> p c r", r=RANK), FFN_SCALE)
            copy(v2s[0][:, :], small[:, 1536:1536 + D], FFN_SCALE)
            copy(u1s[0][:, :, :], small[:, 1792:1792 + DC * RANK].rearrange("p (c r) -> p c r", r=RANK),
                 FFN_SCALE).then_inc(split_hi, 1)
            act.wait_ge(const_in, 80)
            act.wait_ge(set_done, 1)

            def high_x(b, pair):
                act.wait_ge(pe_ln1, at(2 * b + pair + 1))
                copy(xnt[0][:, :, pair * 256:(pair + 1) * 256],
                     t_bank[:, :].rearrange("p (c q) -> p c q", c=DC)).then_inc(hi_ln1, 1)

            high_x(0, 0)
            high_x(0, 1)

            def body(i, mode):
                turn = [0]

                def proj():
                    turn[0] += 1
                    return proj_bank[(turn[0] - 1) % 2]

                def exponentiate(s, n):
                    count = SEG * (i * KV + s - ATT) + n
                    act.wait_ge(pe_scores, at(count + 1))
                    back = 2 if s == 0 and n < 2 else 3
                    if count - back + 1 > 0:
                        act.wait_ge(lo_p, at(count - back + 1))
                    k = SEG * s + n
                    nc.scalar.activation(p_f[:, k % 3, :], score_bank[k % 2][:, :], ACT.Exp).then_inc(exp_done, 1)

                def high_p(s, n):
                    a = i * KV + s - ATT
                    act.wait_ge(exp_done, at(SEG * a + n + 1))
                    if n == 0:
                        if 2 * (a - 1) > 0:
                            act.wait_ge(pe_av, at(2 * (a - 1)))
                    k = (SEG * s + n) % (SEG * KV)
                    copy(p_hi[:, s % 2, n, :], p_f[:, k % 3, :]).then_inc(hi_p, 1)

                for s in range(KV):
                    g = i * KV + s
                    for n in range(SEG):
                        if in_stage(mode, s, ATT):
                            exponentiate(s, n)
                        if n > 0 and in_stage(mode, s, ATT):
                            high_p(s, n - 1)
                        if n == 0 and in_stage(mode, s, ATT + 1):
                            if s > 0:
                                high_p(s - 1, SEG - 1)
                            else:
                                a = i * KV - ATT - 1
                                act.wait_ge(exp_done, at(SEG * (a + 1)))
                                copy(p_hi[:, 1, SEG - 1, :], p_f[:, (SEG * KV - 1) % 3, :]).then_inc(hi_p, 1)
                        if n == 1 and s % 4 == 2 and in_stage(mode, s, 6):
                            gr = i * 4 + (s - 6) // 4
                            act.wait_ge(pe_m, at(gr + 1))
                            q4 = (s - 6) // 4 - 1
                            if 32 * (2 * i + q4 // 2 + 1) > 0:
                                act.wait_ge(m_in[q4 % 2], at(32 * (2 * i + q4 // 2 + 1)))
                            copy(mt[0][:, :], proj()[0:8, :], -1.0).then_inc(hi_m, 1)
                        if n == out_segment(s) and in_stage(mode, s, ATT + 2):
                            a = g - ATT - 2
                            act.wait_ge(pe_ot, at(a + 1))
                            if s == ATT + 2:
                                if 4 * i > 0:
                                    act.wait_ge(pe_op, at(4 * i))
                            copy(ot[0][:, (s - ATT - 2) % KV, :], t_bank[:, :]).then_inc(hi_ot, 1)
                        if (s, n) in X_PAIRS and mode != LAST:
                            if X_PAIRS[s, n] == 0:
                                act.wait_ge(pe_q, at((i + 1) * KV))
                            high_x(i + 1, X_PAIRS[s, n])
                        if n == 0 and s % 2 == 1 and mode != LAST:
                            act.wait_ge(pe_k, at(i * (KV // 2) + (s + 1) // 2))
                            if SEG * (i * KV + s - 7) > 0:
                                act.wait_ge(pe_scores, at(SEG * (i * KV + s - 7)))
                            bank, r0 = proj(), (s - 1) % RING
                            copy(kb[0:HD, r0, :], bank[0:HD, :], KV_OUT)
                            copy(kb[0:HD, r0 + 1, :], bank[HD:P, :], KV_OUT).then_inc(hi_k, 1)
                        if mode != FIRST:
                            if s == 8 and n >= 1:
                                proj()
                            if 9 <= s < 13 and n == 2:
                                u = (i - 1) * 4 + s - 9
                                act.wait_ge(pe_ln2, at(u + 1 + FREE))
                                act.wait_ge(pe_pp, at(u + FREE))
                                copy(x2nt[0][:, :, :], t_bank[:, 0:D].rearrange("p (c q) -> p c q", c=DC)).then_inc(hi_ln2, 1)
                            if (s, n) in FFN_PAIRS:
                                for c in (2 * FFN_PAIRS[s, n], 2 * FFN_PAIRS[s, n] + 1):
                                    act.wait_ge(pe_h, at((i - 1) * FC + c + 1 + FREE))
                                    act.wait_ge(lo_h, at((i - 1) * FC + max(c - 1, 0) + FREE))
                                    nc.scalar.activation(h_f[:, c % 2, :], proj()[:, :], ACT.Gelu_apprx_tanh,
                                                         bias=b1c[:, c:c + 1], scale=1.0 / FFN_SCALE).then_inc(gelu_done, 1)
                            if (s, n) == (15, 0):
                                act.wait_ge(pe_u2, at(i * FC))
                                copy(qf_hi, ffn_bank[:, :], 1.0 / FFN_SCALE).then_inc(hi_qf, 1)
                        if n == 2 and mode != LAST:
                            act.wait_ge(pe_q, at(g + 1))
                            if SEG * (i * KV + s - 7) > 0:
                                act.wait_ge(pe_scores, at(SEG * (i * KV + s - 7)))
                            bank, r = proj(), s % RING
                            copy(qb[0:HD, r, 0, :], bank[0:HD, :], Q_OUT)
                            copy(qb[0:HD, r, 1, :], bank[HD:P, :], Q_OUT).then_inc(hi_q, 1)
                        if n == 4 and s % 8 < 4 and mode != LAST:
                            t, half = s % 8, s // 8
                            act.wait_ge(pe_v, at(i * 8 + half * 4 + t + 1))
                            if 2 * (i * KV + (0 if half else -8)) > 0:
                                act.wait_ge(pe_av, at(2 * (i * KV + (0 if half else -8))))
                            copy(v_hi[:, t, half * 8:(half + 1) * 8, 0:HD],
                                 proj()[:, :].rearrange("p (k d) -> p k d", d=HD), KV_OUT).then_inc(hi_v, 1)
                        if n == 4 and 9 <= s < 13 and mode != FIRST:
                            u = (i - 1) * 4 + s - 9
                            act.wait_ge(pe_pp, at(u + 1 + FREE))
                            if s == 9:
                                act.wait_ge(pe_h, at((i - 1) * FC + FREE))
                            copy(pp[0:RANK, (s - 9) * P:(s - 8) * P], proj()[0:RANK, 0:P], 1.0 / FFN_SCALE).then_inc(hi_pp, 1)

            iterations("act", act, body)

        @block.vector
        def _(dve):
            def low(out_ap, bank, high, scale):
                return nc.vector.scalar_tensor_tensor(out=out_ap, in0=bank, scalar=scale, in1=high,
                                                      op0=ALU.mult, op1=ALU.subtract)

            def ln1(b):
                dve.wait_ge(x_in, at(16 * (b + 1)))
                for t in range(T):
                    last = nc.vector.bn_stats(bst[:, t, :], xt[:, t, :])
                last.then_inc(st1, 1)
                dve.wait_ge(st1, at(b + 1))
                dve.sem_inc(gate, 1)
                for t in range(T):
                    last = nc.vector.bn_aggr(agg[:, t, :], bst[:, t, :])
                last.then_inc(ag1, 1)
                dve.wait_ge(ag1, at(b + 1))
                nc.vector.tensor_scalar(veps[:, :], agg[:, :, 1], EPS, None, ALU.add).then_inc(ve1, 1)
                dve.wait_ge(rs1, at(b + 1))
                for t in range(T):
                    last = nc.vector.tensor_scalar(xt[:, t, :], xt[:, t, :], agg[:, t, 0:1], rstd[:, t:t + 1],
                                                   ALU.subtract, ALU.mult)
                last.then_inc(xn_done, 1)

            dve.sem_inc(y_done, FREE)
            nc.vector.memset(nhalf[:, :], -0.5).then_inc(split_done, 1)
            ln1(0)
            for c, stage in enumerate((qa, qb)):
                dve.wait_ge(split_hi, at(c + 1))
                src = stage[:, :, :, :].rearrange("p a b c -> p (a b c)").bitcast(F32)
                low(wqkv[1][:, c, :], src, wqkv[0][:, c, :], W_SCALE).then_inc(split_done, 1)
            dve.wait_ge(split_hi, 3)
            low(wo[1][:, :, :], ot[0][:, :, :].rearrange("p a b -> p (a b)").bitcast(F32).rearrange("p (c n) -> p c n", n=D),
                wo[0][:, :, :], WO_SCALE)
            dve.wait_ge(split_hi, 4)
            small = ot[1][:, :, :].rearrange("p a b -> p (a b)").bitcast(F32)
            low(v1s[1][:, :], small[:, 0:FF], v1s[0][:, :], FFN_SCALE)
            low(u2s[:, :, RANK:2 * RANK], small[:, 1024:1536].rearrange("p (c r) -> p c r", r=RANK),
                u2s[:, :, 0:RANK], FFN_SCALE)
            low(v2s[1][:, :], small[:, 1536:1536 + D], v2s[0][:, :], FFN_SCALE)
            low(u1s[1][:, :, :], small[:, 1792:1792 + DC * RANK].rearrange("p (c r) -> p c r", r=RANK),
                u1s[0][:, :, :], FFN_SCALE)
            nc.vector.memset(v_hi[:, :, :, HD:HD + 1], 1.0).then_inc(set_done, 1)
            dve.wait_ge(const_in, 80)

            def low_x(b, pair):
                dve.wait_ge(hi_ln1, at(2 * b + pair + 1))
                cols = slice(pair * 256, (pair + 1) * 256)
                low(xnt[1][:, :, cols], t_bank[:, :].rearrange("p (c q) -> p c q", c=DC),
                    xnt[0][:, :, cols], 1.0).then_inc(lo_ln1, 1)

            low_x(0, 0)
            low_x(0, 1)

            def body(i, mode):
                turn = [0]

                def proj():
                    turn[0] += 1
                    return proj_bank[(turn[0] - 1) % 2]

                def maxima(s, n):
                    g = i * KV + s - 2
                    if n == 0 and (s - 2) % 4 == 0:
                        if i * 4 + (s - 2) // 4 - 1 > 0:
                            dve.wait_ge(pe_m, at(i * 4 + (s - 2) // 4 - 1))
                    dve.wait_ge(pe_max, at(SEG * g + n + 1))
                    dve.sem_inc(gate, 1)
                    for h, qt, off in MAX_BLOCKS[n]:
                        bank = max_place(s, n)[0][:, off:off + (qt + 1) * P]
                        col = 2 * ((s - 2) % 4) + h
                        last = nc.vector.tensor_tensor_reduce(
                            out=bank, in0=bank, in1=causal[:, (T - 1 - qt) * P:S], scale=1.0, scalar=-3e38,
                            op0=ALU.add, op1=ALU.max, accum_out=mcol[:, (s - 2) // 4 % 2, qt, col:col + 1])
                    last.then_inc(max_done, 1)

                def normalise(s, h):
                    a = i * KV + s - ATT - 1
                    dve.wait_ge(pe_av, at(2 * a + h + 1))
                    o = o_bank[:, 0:T * (HD + 1)].rearrange("p (t c) -> p t c", t=T)
                    nc.vector.reciprocal(rden[:, h, :], o[:, :, HD]).then_inc(recip_done, 1)
                    if h == 0:
                        if a > 0:
                            dve.wait_ge(pe_ot, at(a))
                    dve.wait_ge(recip_done, at(2 * a + h + 1))
                    nc.vector.tensor_tensor(o_f[:, :, h * HD:(h + 1) * HD], o[:, :, 0:HD],
                                            rden[:, h, :].unsqueeze(2).to_broadcast([P, T, HD]),
                                            ALU.mult).then_inc(o_done, 1)

                for s in range(KV):
                    g = i * KV + s
                    for n in range(SEG):
                        if n == 0 and 9 <= s < 13 and mode != FIRST:
                            t = s - 9
                            u = (i - 1) * 4 + t
                            dve.wait_ge(rs2, at(u + 1))
                            if t == 0:
                                dve.wait_ge(lo_h, at((i - 1) * FC + FREE))
                            dve.wait_ge(pe_ln2, at(u + FREE))
                            nc.vector.tensor_scalar(x2n[:, :], x2[:, t, :], agg2[:, t, 0:1], rstd2[:, t:t + 1],
                                                    ALU.subtract, ALU.mult).then_inc(x2n_done, 1)
                        if n == 1 and s % 4 == 2 and in_stage(mode, s, 6):
                            dve.wait_ge(hi_m, at(i * 4 + (s - 6) // 4 + 1))
                            low(mt[1][:, :], proj()[0:8, :], mt[0][:, :], -1.0).then_inc(lo_m, 1)
                        if in_stage(mode, s, 2):
                            maxima(s, n)
                        if n == 0 and s % 8 in (1, 2, 3, 4) and mode != LAST:
                            t, half = (s - 1) % 8, s // 8
                            heads = slice(half * 8, (half + 1) * 8)
                            dve.wait_ge(hi_v, at(i * 8 + half * 4 + t + 1))
                            low(v_lo[:, t, heads, :], v_bank[:, :].rearrange("p (k d) -> p k d", d=HD),
                                v_hi[:, t, heads, 0:HD], KV_OUT).then_inc(lo_v, 1)
                        if n == 2 * out_segment(s) and in_stage(mode, s, ATT + 2):
                            dve.wait_ge(hi_ot, at(g - ATT - 1))
                            low(ot[1][:, (s - ATT - 2) % KV, :], t_bank[:, :], ot[0][:, (s - ATT - 2) % KV, :],
                                1.0).then_inc(lo_ot, 1)
                        if (s, n) in X_PAIRS and mode != LAST:
                            low_x(i + 1, X_PAIRS[s, n])
                        if n == 1 and s % 2 == 1 and mode != LAST:
                            dve.wait_ge(hi_k, at(i * (KV // 2) + (s + 1) // 2))
                            bank, r0 = proj(), (s - 1) % RING
                            low(ka[0:HD, r0, :], bank[0:HD, :], kb[0:HD, r0, :], KV_OUT)
                            low(ka[0:HD, r0 + 1, :], bank[HD:P, :], kb[0:HD, r0 + 1, :], KV_OUT).then_inc(lo_k, 1)
                        if n == 3 and mode != LAST:
                            dve.wait_ge(hi_q, at(g + 1))
                            bank, r = proj(), s % RING
                            low(qa[HD:P, r, 0, :], bank[0:HD, :], qb[0:HD, r, 0, :], Q_OUT)
                            low(qa[HD:P, r, 1, :], bank[HD:P, :], qb[0:HD, r, 1, :], Q_OUT).then_inc(lo_q, 1)
                        if mode != FIRST:
                            if s == 8 and n >= 1:
                                t = n - 1
                                u = (i - 1) * 4 + t
                                if t == 0:
                                    dve.wait_ge(x2_in, at(16 * i))
                                dve.wait_ge(pe_op, at(u + 1))
                                nc.vector.scalar_tensor_tensor(out=x2[:, t, :], in0=proj()[:, 0:D], scalar=1.0 / WO_SCALE,
                                                               in1=x2[:, t, :], op0=ALU.mult, op1=ALU.add).then_inc(x2_done, 1)
                                dve.wait_ge(x2_done, at(u + 1))
                                nc.vector.bn_stats(bst2[:, t, :], x2[:, t, :]).then_inc(st2, 1)
                                dve.wait_ge(st2, at(u + 1))
                                dve.sem_inc(gate, 1)
                                nc.vector.bn_aggr(agg2[:, t, :], bst2[:, t, :]).then_inc(ag2, 1)
                                dve.wait_ge(ag2, at(u + 1))
                                nc.vector.tensor_scalar(veps2[:, t:t + 1], agg2[:, t, 1:2], EPS, None, ALU.add).then_inc(ve2, 1)
                            if 9 <= s < 13 and n == 2:
                                u = (i - 1) * 4 + s - 9
                                dve.wait_ge(hi_ln2, at(u + 1))
                                low(x2nt[1][:, :, :], t_bank[:, 0:D].rearrange("p (c q) -> p c q", c=DC),
                                    x2nt[0][:, :, :], 1.0).then_inc(lo_ln2, 1)
                            if (s, n) in FFN_PAIRS:
                                for c in (2 * FFN_PAIRS[s, n], 2 * FFN_PAIRS[s, n] + 1):
                                    proj()
                                    dve.wait_ge(gelu_done, at((i - 1) * FC + c + 1))
                                    if c >= 2:
                                        dve.wait_ge(pe_u2, at((i - 1) * FC + c - 1))
                                    elif c == 0:
                                        dve.wait_ge(pe_y, at(2 * (i - 1) + FREE))
                                    nc.vector.tensor_copy(h_hi[:, c % 2, :], h_f[:, c % 2, :]).then_inc(hi_h, 1)
                            if (s, n) == (15, 0):
                                dve.wait_ge(hi_qf, at(i))
                                low(qf_lo, ffn_bank[:, :], qf_hi, 1.0 / FFN_SCALE).then_inc(lo_qf, 1)
                            if (s, n) in Y_PAIRS:
                                pair = Y_PAIRS[s, n]
                                dve.wait_ge(pe_y, at(2 * (i - 1) + pair + 1 + FREE))
                                if pair == 0:
                                    dve.wait_ge(b2_done, at(4 * i))
                                rows = x2[:, 2 * pair:2 * pair + 2, :]
                                nc.vector.scalar_tensor_tensor(out=rows, in0=ffn_bank[:, :].rearrange("p (t d) -> p t d", d=D),
                                                               scalar=1.0 / FFN_SCALE, in1=rows, op0=ALU.mult,
                                                               op1=ALU.add).then_inc(y_done, 1)
                        if n in (1, 3) and in_stage(mode, s, ATT + 1):
                            normalise(s, n // 2)
                        if n == 4 and s % 8 < 4 and mode != LAST:
                            v_bank = proj()
                        if n == 4 and 9 <= s < 13 and mode != FIRST:
                            dve.wait_ge(hi_pp, at((i - 1) * 4 + s - 8))
                            cols = slice((s - 9) * P, (s - 8) * P)
                            low(pp[RANK:P, cols], proj()[0:RANK, 0:P], pp[0:RANK, cols], 1.0 / FFN_SCALE).then_inc(lo_pp, 1)
                    if s == 7 and mode != LAST:
                        ln1(i + 1)

            iterations("dve", dve, body)

        @block.gpsimd
        def _(pool):
            pool.sem_inc(lo_h, FREE)
            pool.wait_ge(split_done, 1)

            def power1(b):
                pool.wait_ge(ve1, at(b + 1))
                nc.gpsimd.tensor_tensor(rstd[:, :], veps[:, :], nhalf[:, :], ALU.pow).then_inc(rs1, 1)

            power1(0)
            pool.wait_ge(rs1, 1)
            nc.gpsimd.memset(kb[HD:P, :, :], 0.0).then_inc(k_rows, 1)
            pool.wait_ge(k_rows, 1)
            nc.gpsimd.memset(kb[MAX0:MAX0 + 2, :, :], 1.0).then_inc(k_rows, 1)
            pool.wait_ge(k_rows, 2)
            pool.wait_ge(split_done, 3)
            nc.gpsimd.memset(qb[HD:P, :, :, :], 0.0).then_inc(zeroed, 1)
            pool.wait_ge(zeroed, 1)

            def body(i, mode):
                def low_p(count, slot, n, k):
                    pool.wait_ge(hi_p, at(count + 1))
                    nc.gpsimd.tensor_tensor(p_lo[:, slot, n, :], p_f[:, k % 3, :], p_hi[:, slot, n, :],
                                            ALU.subtract).then_inc(lo_p, 1)

                for s in range(KV):
                    for n in range(SEG):
                        if n > 0 and in_stage(mode, s, ATT):
                            low_p(SEG * (i * KV + s - ATT) + n - 1, s % 2, n - 1, SEG * s + n - 1)
                        if n == 0 and in_stage(mode, s, ATT + 1):
                            low_p(SEG * (i * KV + s - ATT) - 1, (s - 1) % 2, SEG - 1, (SEG * s - 1) % (SEG * KV))
                        if mode != FIRST:
                            if s == 8 and n >= 1:
                                t = n - 1
                                pool.wait_ge(ve2, at((i - 1) * 4 + t + 1))
                                nc.gpsimd.tensor_tensor(rstd2[:, t:t + 1], veps2[:, t:t + 1], nhalf[:, 0:1],
                                                        ALU.pow).then_inc(rs2, 1)
                            if 9 <= s < 13 and n == 1:
                                t = s - 9
                                pool.wait_ge(x2n_done, at((i - 1) * 4 + t + 1))
                                nc.gpsimd.tensor_tensor(x2[:, t, :], x2[:, t, :], b2b[:, :], ALU.add).then_inc(b2_done, 1)
                            if (s, n) in FFN_PAIRS:
                                for c in (2 * FFN_PAIRS[s, n], 2 * FFN_PAIRS[s, n] + 1):
                                    pool.wait_ge(hi_h, at((i - 1) * FC + c + 1))
                                    nc.gpsimd.tensor_tensor(h_lo[:, c % 2, :], h_f[:, c % 2, :], h_hi[:, c % 2, :],
                                                            ALU.subtract).then_inc(lo_h, 1)
                    if s == 7 and mode != LAST:
                        power1(i + 1)

            pool.wait_ge(const_in, 80)
            iterations("pool", pool, body)


_NAMES = ["L0_attn_inputs", "L0_attn_W_qkv", "L0_attn_W_out", "L0_ffn_U1", "L0_ffn_V1", "L0_ffn_b1",
          "L0_ffn_U2", "L0_ffn_V2", "L0_ffn_b2"]


def constants():
    import numpy as np

    slope = (np.float64(2.0) ** -0.25) ** np.arange(1, 2 * KV + 1)
    slope = slope.astype(np.float32).astype(np.float64)
    s1 = slope.astype(np.float16).astype(np.float64)
    s2 = (slope - s1).astype(np.float16).astype(np.float64)
    pos = np.arange(S, dtype=np.float64)
    sk = (s1 + s2)[:, None] * pos[None, :]
    parts = []
    for _ in range(3):
        part = sk.astype(np.float16).astype(np.float64)
        parts.append(part)
        sk = sk - part
    k_aug = np.zeros((AUG, KV, S), np.float16)
    q_aug = np.zeros((AUG, RING, 2, S), np.float16)
    for h in range(2):
        rows = [parts[0][h::2], np.broadcast_to(-s1[h::2, None], (KV, S)), parts[1][h::2],
                np.broadcast_to(-s2[h::2, None], (KV, S)), parts[2][h::2]]
        for j, row in enumerate(rows):
            k_aug[5 * h + j] = row.astype(np.float16)
            q_aug[5 * h + j, :, h, :] = (pos if j in (1, 3) else np.ones(S)).astype(np.float16)
    ident = np.eye(P, dtype=np.float32)
    causal = np.zeros((P, S), np.float32)
    causal[:, S - P:] = np.where(np.arange(P)[None, :] > np.arange(P)[:, None], np.float32(-1e30), np.float32(0))
    return k_aug, q_aug.reshape(AUG, RING * 2 * S), ident, causal


def kernel(**inputs):
    import ml_dtypes
    import numpy as _np
    import concourse.bacc as _bacc
    from concourse import mybir as _mybir
    from concourse.bass_utils import run_bass_kernel_spmd as _run

    nc = _bacc.Bacc("TRN2", target_bir_lowering=False, num_devices=1)
    arrays, args = {}, []
    k_aug, q_aug, ident, causal = constants()
    consts = {"k_aug": k_aug, "q_aug": q_aug, "ident": ident, "ident_b": ident.astype(ml_dtypes.bfloat16), "causal": causal.astype(ml_dtypes.bfloat16)}
    for name, a in [(n, inputs[n]) for n in _NAMES] + list(consts.items()):
        if name == "L0_ffn_b1":
            a = _np.asarray(a).reshape(FC, P).T
        a = _np.ascontiguousarray(a)
        arrays[f"in_{name}"] = a
        args.append(nc.dram_tensor(f"in_{name}", a.shape, _mybir.dt.from_np(a.dtype), kind="ExternalInput").ap())
    out = nc.dram_tensor("out_0", inputs["L0_attn_inputs"].shape, F32, kind="ExternalOutput").ap()
    layer(nc, *args, out)
    r = _run(nc, [arrays], core_ids=[0])
    return r.results[0]["out_0"]
```

```python
from contextlib import ExitStack

import concourse.bass as bass
from concourse import mybir

F32 = mybir.dt.float32
F16 = mybir.dt.float16
BF16 = mybir.dt.bfloat16
ALU = mybir.AluOpType
ACT = mybir.ActivationFunctionType

P = 128
D = 256
DC = D // P
S = 512
T = S // P
HD = 64
KV = 16
QD = 2 * KV * HD
KD = KV * HD
FF = 1024
FC = FF // P
RANK = 64
RING = 8
SEG = 5
AUG = 10
AUG0, MAX0 = 64, 96
ATT = 7
EPS = 1e-5
W_SCALE, WO_SCALE, FFN_SCALE = 16.0, 32.0, 8.0
Q_OUT = 1.0 / (W_SCALE * 8.0)
KV_OUT = 1.0 / W_SCALE

SCORE_BLOCKS = [[(0, 0, 0, 512)], [(1, 0, 0, 512)],
                [(0, 1, 0, 384), (0, 3, 384, 128)], [(1, 1, 0, 384), (1, 3, 384, 128)],
                [(0, 2, 0, 256), (1, 2, 256, 256)]]
P_AT = {(h, kt): (n, off) for n, blocks in enumerate(SCORE_BLOCKS) for h, kt, off, _ in blocks}
MAX_BLOCKS = [[(0, 3, 0)], [(0, 2, 0), (0, 0, 384)], [(0, 1, 0), (1, 1, 256)],
              [(1, 3, 0)], [(1, 2, 0), (1, 0, 384)]]
MAX_SEG, K_SEG, V_SEG = 1, 0, 4
LN2_SEG, U1_SEG = 2, 3
FFN_PAIRS = {(13, 1): 0, (13, 3): 1, (13, 4): 2, (14, 3): 3}
U2_PAIRS = {(13, 3): 0, (14, 0): 1, (14, 1): 2, (15, 1): 3}
U2_START = 13 * SEG + 3
QF_AT, Y_AT = (15, 2), (15, 4)
X_PAIRS = {(15, 3): 0, (15, 4): 1}


def before(s, n, lag):
    return divmod(SEG * s + n - lag, SEG)


def in_ffn_bank(k):
    return k % 2 == 1 and k < U2_START


def q_segment(s):
    return 2 if s % 2 else 1


def out_segment(s):
    return 0


def q_lag(s):
    return 1


def k_lag(s):
    return 1


def v_lag(s):
    return 1 if s >= 8 else 0


def out_lag(s):
    return 0


def projection_order():
    uses = []
    for s in range(KV):
        for n in range(SEG):
            if n == MAX_SEG and s % 4 == 2:
                uses.append(("max", s))
            if n == K_SEG and s % 2 == 1:
                uses.append(("k", s))
            if s == 8 and n >= 1:
                uses.append(("out", n - 1))
            if (s, n) in FFN_PAIRS:
                uses += [("h", 2 * FFN_PAIRS[s, n]), ("h", 2 * FFN_PAIRS[s, n] + 1)]
            if n == q_segment(s):
                uses.append(("q", s))
            if n == V_SEG and s % 8 < 4:
                uses.append(("v", s))
            if n == U1_SEG and 9 <= s < 13:
                uses.append(("p", s - 9))
            if (s, n) == Y_AT:
                uses += [("y", 0), ("y", 1)]
    return uses


PROJ = {use: k % 2 for k, use in enumerate(projection_order())}

MULTIPLES = (1, 2, 4, 8, 16, 32, 64, 80)

FREE = 1

FIRST, MID, LAST = "first", "mid", "last"


class Count:

    def __init__(self, i, regs=None, times=1, plus=0):
        self.i, self.regs, self.times, self.plus = i, regs, times, plus

    def __add__(self, n):
        return Count(self.i, self.regs, self.times, self.plus + n)

    __radd__ = __add__

    def __sub__(self, n):
        return self + -n

    def __mul__(self, n):
        return Count(self.i, self.regs, self.times * n, self.plus * n)

    __rmul__ = __mul__

    def __gt__(self, n):
        return bool(self.regs) or self.value() > n

    def value(self):
        return self.i * self.times + self.plus


def in_stage(mode, s, lag):
    return s >= lag if mode == FIRST else s < lag if mode == LAST else True


def layer(nc, x, w_qkv, w_out, u1, v1, b1, u2, v2, b2, k_aug, q_aug, ident_d, ident_b_d, causal_d, out):
    B = x.shape[0]
    ctx = ExitStack()
    with ctx:
        def sb(name, shape, dt):
            return ctx.enter_context(nc.sbuf_tensor(name, shape, dt))

        def psum(name):
            return ctx.enter_context(nc.psum_tensor(name, [P, 512], F32))

        def sem(name):
            return ctx.enter_context(nc.semaphore(name))

        wqkv = [sb(f"wqkv_{p}", [P, DC, QD + 2 * KD], F16) for p in ("hi", "lo")]
        wo = [sb(f"wo_{p}", [P, KV, D], F16) for p in ("hi", "lo")]
        u1s = [sb(f"u1_{p}", [P, DC, RANK], F16) for p in ("hi", "lo")]
        v1s = [sb(f"v1_{p}", [P, FF], F16) for p in ("hi", "lo")]
        v2s = [sb(f"v2_{p}", [P, D], F16) for p in ("hi", "lo")]
        u2s = sb("u2_hi_lo", [P, FC, 2 * RANK], F16)
        b1c = sb("b1_cols", [P, FC], F32)
        b2b = sb("b2_rows", [P, D], F32)
        ident = sb("ident", [P, P], F32)
        ident_b = sb("ident_bf16", [P, P], BF16)
        causal = sb("causal", [P, S], BF16)
        nhalf = sb("nhalf", [P, T], F32)
        qa = sb("q_hi_lo", [P, RING, 2, S], F16)
        qb = sb("q_hi_aug", [P, RING, 2, S], F16)
        ka = sb("k_lo_hi", [P, RING, S], F16)
        kb = sb("k_hi_aug", [P, RING, S], F16)
        v_hi = sb("v_hi_one", [P, T, KV, HD + 1], F16)
        v_lo = sb("v_lo", [P, T, KV, HD], F16)
        p_f = sb("p_f32", [P, 3, 512], F32)
        p_hi = sb("p_hi", [P, 2, SEG, 512], F16)
        p_lo = sb("p_lo", [P, 2, SEG, 512], F16)
        o_f = sb("o_f32", [P, T, 2 * HD], F32)
        rden = sb("rden", [P, 2, T], F32)
        ot = [sb(f"o_t_{p}", [P, KV, S], F16) for p in ("hi", "lo")]
        mcol = sb("row_max", [P, 2, T, 8], F32)
        mt = [sb(f"neg_max_t_{p}", [8, S], F16) for p in ("hi", "lo")]
        xt = sb("x_rows", [P, T, D], F32)
        xnt = [sb(f"xn_t_{p}", [P, DC, S], F16) for p in ("hi", "lo")]
        bst = sb("bn_stats", [P, T, 6], F32)
        agg = sb("bn_aggr", [P, T, 2], F32)
        veps = sb("var_eps", [P, T], F32)
        rstd = sb("rstd", [P, T], F32)
        x2 = sb("x2_rows", [P, T, D], F32)
        bst2 = sb("bn_stats2", [P, T, 6], F32)
        agg2 = sb("bn_aggr2", [P, T, 2], F32)
        veps2 = sb("var_eps2", [P, T], F32)
        rstd2 = sb("rstd2", [P, T], F32)
        x2nt = [sb(f"x2n_t_{p}", [P, DC, P], F16) for p in ("hi", "lo")]
        pp = sb("ffn_p_hi_lo", [P, S], F16)
        h_f = sb("h_f32", [P, 2, S], F32)
        x2n = h_f[:, 0, 0:D]
        h_hi = sb("h_hi", [P, 2, S], F16)
        h_lo = sb("h_lo", [P, 2, S], F16)
        qf_hi, qf_lo = h_hi[:, 0, :], h_lo[:, 0, :]

        score_bank = [psum("scores0"), psum("scores1")]
        max_bank = psum("max_scores")
        o_bank = psum("o_acc")
        proj_bank = [psum("proj0"), psum("proj1")]
        t_bank = psum("transposes")
        ffn_bank = psum("ffn_acc")

        w_in = [sem(f"w_in{n}") for n in range(4)]
        ident_in, const_in, split_hi, split_done, set_done = sem("ident_in"), sem("const_in"), sem("split_hi"), sem("split_done"), sem("set_done")
        zeroed, qaug_in, x_in, k_rows = sem("zeroed"), sem("qaug_in"), sem("x_in"), sem("k_rows_set")
        x2_in, y_out = sem("x2_in"), sem("y_out")
        qdup_in = [sem(f"qdup_in{r}") for r in range(RING)]
        kdup_in = [sem(f"kdup_in{r}") for r in range(RING // 2)]
        kaug_in = [sem(f"kaug_in{r}") for r in range(RING // 2)]
        m_in = [sem("m_in0"), sem("m_in1")]
        pe_scores, pe_max, pe_av, pe_ot, pe_m = sem("pe_scores"), sem("pe_max"), sem("pe_av"), sem("pe_ot"), sem("pe_m")
        pe_ln1, pe_ln2, pe_q, pe_k, pe_v = sem("pe_ln1"), sem("pe_ln2"), sem("pe_q"), sem("pe_k"), sem("pe_v")
        pe_op, pe_pp, pe_h, pe_u2, pe_y = sem("pe_op"), sem("pe_pp"), sem("pe_h"), sem("pe_u2"), sem("pe_y")
        hi_q, hi_k, hi_v, hi_ot, hi_m = sem("hi_q"), sem("hi_k"), sem("hi_v"), sem("hi_ot"), sem("hi_m")
        hi_ln1, hi_ln2, hi_pp, hi_qf = sem("hi_ln1"), sem("hi_ln2"), sem("hi_pp"), sem("hi_qf")
        exp_done, hi_p, lo_p = sem("exp_done"), sem("hi_p"), sem("lo_p")
        gelu_done, hi_h, lo_h = sem("gelu_done"), sem("hi_h"), sem("lo_h")
        max_done, lo_q, lo_k, lo_v, lo_ot, lo_m = sem("max_done"), sem("lo_q"), sem("lo_k"), sem("lo_v"), sem("lo_ot"), sem("lo_m")
        lo_ln1, lo_ln2, lo_pp, lo_qf = sem("lo_ln1"), sem("lo_ln2"), sem("lo_pp"), sem("lo_qf")
        recip_done, o_done, y_done, b2_done = sem("recip_done"), sem("o_done"), sem("y_done"), sem("b2_done")
        st1, ag1, ve1, rs1, xn_done = sem("ln1_stats"), sem("ln1_aggr"), sem("ln1_veps"), sem("ln1_rstd"), sem("ln1_done")
        x2_done, st2, ag2, ve2, rs2, x2n_done = sem("x2_done"), sem("ln2_stats"), sem("ln2_aggr"), sem("ln2_veps"), sem("ln2_rstd"), sem("ln2_done")

        gate = sem("gate")

        block = ctx.enter_context(nc.Block())

        def at(count):
            if not isinstance(count, Count):
                return count
            if not count.regs:
                return count.value()
            if not count.plus:
                return count.regs[count.times]
            count.regs["eng"].reg_add(count.regs["target"], count.regs[count.times], count.plus)
            return count.regs["target"]

        def max_place(s, n):
            k, total = SEG * s + n, SEG * KV
            back = next(j for j in range(1, total) if in_ffn_bank((k - j) % total) == in_ffn_bank(k))
            return (ffn_bank if in_ffn_bank(k) else max_bank), back

        def iterations(name, eng, body):
            body(Count(0), FIRST)
            regs = {n: eng.alloc_register(f"{name}_{n}") for n in (*MULTIPLES, "target")}
            regs["eng"] = eng
            with eng.Fori(1, B) as i:
                for times in MULTIPLES:
                    eng.reg_mul(regs[times], i, times)
                body(Count(i, regs), MID)
            body(Count(B), LAST)

        def x_src(b):
            return x[b].rearrange("(t p) d -> p t d", p=P)

        @block.sync
        def _(sp):
            sp.sem_inc(y_out, FREE)
            stage = [qa, qb]
            sp.dma_start(xt[:, :, :], x_src(0)).then_inc(x_in, 16)
            sp.dma_start(ident[:, :], ident_d).then_inc(ident_in, 16)
            for c in range(DC):
                sp.dma_start(stage[c][:, :, :, :].rearrange("p a b c -> p (a b c)").bitcast(F32),
                             w_qkv[c * P:(c + 1) * P, :]).then_inc(w_in[c], 16)
            sp.dma_start(ot[0][:, :, :].rearrange("p a b -> p (a b)").bitcast(F32).rearrange("p (c n) -> p c n", n=D),
                         w_out.rearrange("(c p) n -> p c n", p=P)).then_inc(w_in[2], 16)
            small = ot[1][:, :, :].rearrange("p a b -> p (a b)").bitcast(F32)
            for r in range(2):
                rows = slice(r * RANK, (r + 1) * RANK)
                sp.dma_start(small[rows, 0:FF], v1).then_inc(w_in[3], 16)
                sp.dma_start(small[rows, 1536:1536 + D], v2).then_inc(w_in[3], 16)
            sp.dma_start(small[:, 1024:1536].rearrange("p (c r) -> p c r", r=RANK),
                         u2.rearrange("(c p) r -> p c r", p=P)).then_inc(w_in[3], 16)
            sp.dma_start(small[:, 1792:1792 + DC * RANK].rearrange("p (c r) -> p c r", r=RANK),
                         u1.rearrange("(c p) r -> p c r", p=P)).then_inc(w_in[3], 16)
            sp.dma_start(causal[:, :], causal_d).then_inc(const_in, 16)
            sp.dma_start(ident_b[:, :], ident_b_d).then_inc(const_in, 16)
            sp.dma_start(b1c[:, :], b1).then_inc(const_in, 16)
            sp.dma_start(b2b[:, :], b2.rearrange("(o d) -> o d", o=1).to_broadcast([P, D])).then_inc(const_in, 16)
            sp.wait_ge(zeroed, 1)
            sp.wait_ge(k_rows, 2)
            sp.dma_start(qb[AUG0:AUG0 + AUG, :, :, :].rearrange("p a b c -> p (a b c)"), q_aug).then_inc(qaug_in, 16)

            def body(i, mode):
                for s in range(KV):
                    g = i * KV + s
                    if s % 4 == 2 and in_stage(mode, s, 6):
                        gr = i * 4 + (s - 6) // 4
                        sp.wait_ge(lo_m, at(gr + 1))
                        r0 = (s - 6) % RING
                        for part in range(2):
                            sp.dma_start(qb[MAX0 + part:MAX0 + part + 1, r0:r0 + 4, :, :].rearrange("o a b q -> o (a b) q"),
                                         mt[part][:, :]).then_inc(m_in[(s - 6) // 4 % 2], 16)
                    if mode != LAST:
                        if s % 2 == 1:
                            r0 = (s - 1) % RING
                            if SEG * (i * KV + s - 7) > 0:
                                sp.wait_ge(pe_scores, at(SEG * (i * KV + s - 7)))
                            sp.dma_start(kb[AUG0:AUG0 + AUG, r0:r0 + 2, :],
                                         k_aug[:, s - 1:s + 1, :]).then_inc(kaug_in[r0 // 2], 16)
                            sp.wait_ge(hi_k, at(i * (KV // 2) + (s + 1) // 2))
                            sp.dma_start(ka[HD:P, r0:r0 + 2, :], kb[0:HD, r0:r0 + 2, :]).then_inc(kdup_in[r0 // 2], 16)
                        sp.wait_ge(hi_q, at(g + 1))
                        r = s % RING
                        sp.dma_start(qa[0:HD, r, :, :], qb[0:HD, r, :, :]).then_inc(qdup_in[r], 16)
                    if s == 2 and mode != FIRST:
                        sp.wait_ge(y_out, at(16 * (i - 1) + FREE))
                        sp.dma_start(x2[:, :, :], x_src((i - 1).value())).then_inc(x2_in, 16)
                    if s == 4 and mode != LAST:
                        sp.wait_ge(pe_ln1, at(2 * (i + 1)))
                        sp.dma_start(xt[:, :, :], x_src((i + 1).value() % B)).then_inc(x_in, 16)
                if mode != FIRST:
                    sp.wait_ge(y_done, at(2 * i + FREE))
                    sp.dma_start(out[(i - 1).value()].rearrange("(t p) d -> p t d", p=P), x2[:, :, :]).then_inc(y_out, 16)

            iterations("sp", sp, body)
            sp.wait_ge(y_out, 16 * B + FREE)
            sp.wait_ge(x_in, 16 * (B + 1))

        @block.tensor
        def _(pe):
            pe.sem_inc(pe_pp, FREE)
            pe.sem_inc(pe_h, FREE)
            pe.sem_inc(pe_ln2, FREE)
            pe.sem_inc(pe_y, FREE)

            def mm(out_ap, lhs, rhs, start, stop):
                return nc.tensor.matmul(out_ap, lhs, rhs, start=start, stop=stop, skip_group_check=True)

            def split_mm(out_ap, lhs, rhs, first=True, last=True):
                mm(out_ap, lhs[1], rhs[0], first, False)
                mm(out_ap, lhs[0], rhs[1], False, False)
                return mm(out_ap, lhs[0], rhs[0], False, last)

            pe.wait_ge(ident_in, 16)

            def transpose_x(b, pair):
                if pair == 0:
                    pe.wait_ge(xn_done, at(b + 1))
                for c in range(DC):
                    for t in range(2):
                        col = (c * 2 + t) * P
                        last = nc.tensor.transpose(t_bank[:, col:col + P], xt[:, 2 * pair + t, c * P:(c + 1) * P], ident[:, :])
                last.then_inc(pe_ln1, 1)

            transpose_x(0, 0)
            pe.wait_ge(lo_ln1, 1)
            transpose_x(0, 1)
            pe.wait_ge(split_done, 3)

            def body(i, mode):
                proj_free = [(lo_q, i * KV), (lo_q, i * KV)]
                t_free = [(lo_ln1, 2 * (i + 1))]

                def next_proj(use, semaphore, count):
                    b = PROJ[use]
                    read, times = proj_free[b]
                    if times > 0:
                        pe.wait_ge(read, at(times))
                    proj_free[b] = (semaphore, count)
                    return proj_bank[b]

                def transposes_bank(semaphore, count):
                    read, times = t_free[0]
                    if times > 0:
                        pe.wait_ge(read, at(times))
                    t_free[0] = (semaphore, count)
                    return t_bank

                def scores(s, n):
                    a = i * KV + s - ATT
                    r = (s - ATT) % RING
                    if n == 0:
                        use = 2 * i + (s - ATT) // RING + 1
                        pe.wait_ge(qdup_in[r], at(16 * use))
                        pe.wait_ge(lo_q, at(a + 1))
                        if (s - ATT) % 2 == 0:
                            pe.wait_ge(kdup_in[r // 2], at(16 * use))
                            pe.wait_ge(lo_k, at(i * (KV // 2) + (s - ATT) // 2 + 1))
                        if (s - ATT) % 4 == 0:
                            q4 = (s - ATT) // 4
                            pe.wait_ge(m_in[q4 % 2], at(32 * (2 * i + q4 // 2 + 1)))
                    if SEG * a + n - 1 > 0:
                        pe.wait_ge(exp_done, at(SEG * a + n - 1))
                    bank = score_bank[(SEG * s + n) % 2]
                    for h, kt, off, width in SCORE_BLOCKS[n]:
                        keys = slice(kt * P, (kt + 1) * P)
                        o = bank[:, off:off + width]
                        mm(o, ka[:, r, keys], qa[:, r, h, kt * P:S], True, False)
                        mm(o[:, 0:P], causal[:, S - P:S], ident_b[:, :], False, False)
                        last = mm(o, kb[:, r, keys], qb[:, r, h, kt * P:S], False, True)
                    last.then_inc(pe_scores, 1)

                def max_scores(s, n):
                    g = i * KV + s - 2
                    r = (s - 2) % RING
                    if n == 0:
                        pe.wait_ge(hi_q, at(g + 1))
                        if s % 2 == 0:
                            pe.wait_ge(hi_k, at(i * (KV // 2) + (s - 2) // 2 + 1))
                            pe.wait_ge(kaug_in[r // 2], at(16 * (2 * i + (s - 2) // RING + 1)))
                    bank, back = max_place(s, n)
                    if (s, n) == (0, 1) and mode != FIRST:
                        pe.wait_ge(lo_qf, at(i - 1 + FREE))
                        pe.wait_ge(y_done, at(2 * (i - 1) + FREE))
                    if SEG * g + n + 1 - back > 0:
                        pe.wait_ge(max_done, at(SEG * g + n + 1 - back))
                    for h, qt, off in MAX_BLOCKS[n]:
                        width = (qt + 1) * P
                        last = mm(bank[:, off:off + width], qb[0:MAX0, r, h, qt * P:(qt + 1) * P],
                                  kb[0:MAX0, r, 0:width], True, True)
                    last.then_inc(pe_max, 1)

                def transpose_max(s):
                    gr = i * 4 + (s - 6) // 4
                    bank = next_proj(("max", s), lo_m, gr + 1)
                    pe.wait_ge(max_done, at(4 * SEG * (gr + 1)))
                    for qt in range(T):
                        last = nc.tensor.transpose(bank[0:8, qt * P:(qt + 1) * P], mcol[:, (s - 6) // 4 % 2, qt, :], ident[:, :])
                    last.then_inc(pe_m, 1)

                def attend(s, h):
                    a = i * KV + s - ATT - 1
                    kv, slot = (s - ATT - 1) % KV, (s - 1) % 2
                    if h == 0:
                        pe.wait_ge(lo_p, at(SEG * (a + 1)))
                        if kv % 8 == 0:
                            pe.wait_ge(lo_v, at(i * 8 + (4 if kv == 0 else 0)))
                    if 2 * a + h > 0:
                        pe.wait_ge(o_done, at(2 * a + h))
                    first = True
                    for qt in range(T):
                        for kt in range(qt + 1):
                            n, off = P_AT[h, kt]
                            cols = slice(off + (qt - kt) * P, off + (qt - kt + 1) * P)
                            o = o_bank[:, qt * (HD + 1):(qt + 1) * (HD + 1)]
                            mm(o, p_lo[:, slot, n, cols], v_hi[:, kt, kv, :], kt == 0, False)
                            mm(o[:, 0:HD], p_hi[:, slot, n, cols], v_lo[:, kt, kv, :], False, False)
                            last = mm(o, p_hi[:, slot, n, cols], v_hi[:, kt, kv, :], False, kt == qt)
                    last.then_inc(pe_av, 1)

                def transpose_o(s):
                    a = i * KV + s - ATT - 2
                    bank = transposes_bank(lo_ot, a + 1)
                    pe.wait_ge(o_done, at(2 * (a + 1)))
                    for qt in range(T):
                        last = nc.tensor.transpose(bank[:, qt * P:(qt + 1) * P], o_f[:, qt, :], ident[:, :])
                    last.then_inc(pe_ot, 1)

                def project(bank, col, semaphore):
                    for c in range(DC):
                        last = split_mm(bank[:, :], [w[:, c, col:col + P] for w in wqkv],
                                        [v[:, c, :] for v in xnt], c == 0, c == DC - 1)
                    last.then_inc(semaphore, 1)

                def project_v(s):
                    t, half = s % 8, s // 8
                    bank = next_proj(("v", s), lo_v, i * 8 + half * 4 + t + 1)
                    col = QD + KD + half * 512
                    for c in range(DC):
                        last = split_mm(bank[:, :], [v[:, c, t * P:(t + 1) * P] for v in xnt],
                                        [w[:, c, col:col + 512] for w in wqkv], c == 0, c == DC - 1)
                    last.then_inc(pe_v, 1)

                def project_out(t):
                    bank = next_proj(("out", t), x2_done, (i - 1) * 4 + t + 1)
                    for kv in range(KV):
                        if t == 0 and kv == KV - 1:
                            pe.wait_ge(lo_ot, at(i * KV))
                        last = split_mm(bank[:, 0:D], [o[:, kv, t * P:(t + 1) * P] for o in ot],
                                        [w[:, kv, :] for w in wo], kv == 0, kv == KV - 1)
                    last.then_inc(pe_op, 1)

                def transpose_x2(t):
                    u = (i - 1) * 4 + t
                    bank = transposes_bank(lo_ln2, u + 1)
                    pe.wait_ge(x2n_done, at(u + 1))
                    for c in range(DC):
                        last = nc.tensor.transpose(bank[:, c * P:(c + 1) * P], x2n[:, c * P:(c + 1) * P], ident[:, :])
                    last.then_inc(pe_ln2, 1)

                def ffn_p(t):
                    u = (i - 1) * 4 + t
                    bank = next_proj(("p", t), lo_pp, u + 1)
                    pe.wait_ge(lo_ln2, at(u + 1))
                    for c in range(DC):
                        last = split_mm(bank[0:RANK, 0:P], [w[:, c, :] for w in u1s],
                                        [v[:, c, :] for v in x2nt], c == 0, c == DC - 1)
                    last.then_inc(pe_pp, 1)

                def ffn_h(pair):
                    for c in (2 * pair, 2 * pair + 1):
                        bank = next_proj(("h", c), gelu_done, (i - 1) * FC + c + 1)
                        if c == 0:
                            pe.wait_ge(lo_pp, at(4 * i))
                        mm(bank[:, :], v1s[1][:, c * P:(c + 1) * P], pp[:, :], True, False)
                        mm(bank[:, :], v1s[0][:, c * P:(c + 1) * P], pp[:, :], False, True).then_inc(pe_h, 1)

                def ffn_u2(pair):
                    for c in (2 * pair, 2 * pair + 1):
                        if c == 0 and mode != LAST:
                            pe.wait_ge(max_done, at(SEG * (i * KV - 2) + U2_START))
                        pe.wait_ge(hi_h, at((i - 1) * FC + c + 1))
                        mm(ffn_bank[:, :], u2s[:, c, :], h_hi[:, c % 2, :], c == 0, False)
                        pe.wait_ge(lo_h, at((i - 1) * FC + c + 1 + FREE))
                        mm(ffn_bank[:, :], u2s[:, c, :], h_lo[:, c % 2, :], False, c == FC - 1).then_inc(pe_u2, 1)

                def ffn_y(pair):
                    bank = next_proj(("y", pair), y_done, 2 * (i - 1) + pair + 1 + FREE)
                    if pair == 0:
                        pe.wait_ge(lo_qf, at(i + FREE))
                    for t in range(2):
                        tok = slice((2 * pair + t) * P, (2 * pair + t + 1) * P)
                        last = split_mm(bank[:, t * D:(t + 1) * D], [qf_hi[:, tok], qf_lo[:, tok]],
                                        [v[:, :] for v in v2s])
                    last.then_inc(pe_y, 1)

                for s in range(KV):
                    if mode == FIRST and s == 2:
                        pe.wait_ge(k_rows, 2)
                        pe.wait_ge(qaug_in, 16)
                    if mode == FIRST and s == 6:
                        pe.wait_ge(const_in, 64)
                    if mode == FIRST and s == 8:
                        pe.wait_ge(set_done, 1)
                    for n in range(SEG):
                        if in_stage(mode, s, ATT):
                            scores(s, n)
                        if n == MAX_SEG and s % 4 == 2 and in_stage(mode, s, 6):
                            transpose_max(s)
                        if in_stage(mode, s, 2):
                            max_scores(s, n)
                        if n == out_segment(s) and in_stage(mode, s, ATT + 2):
                            transpose_o(s)
                        if (s, n) in X_PAIRS and mode != LAST:
                            pair = X_PAIRS[s, n]
                            transposes_bank(lo_ln1, 2 * (i + 1) + pair + 1)
                            transpose_x(i + 1, pair)
                        if n == K_SEG and s % 2 == 1 and mode != LAST:
                            pair = (s - 1) // 2
                            project(next_proj(("k", s), lo_k, i * (KV // 2) + pair + 1), QD + pair * P, pe_k)
                        if mode != FIRST:
                            if s == 8 and n >= 1:
                                project_out(n - 1)
                            if 9 <= s < 13 and n == LN2_SEG:
                                transpose_x2(s - 9)
                            if (s, n) in FFN_PAIRS:
                                ffn_h(FFN_PAIRS[s, n])
                        if n == q_segment(s) and mode != LAST:
                            if s == 0:
                                pe.wait_ge(lo_ln1, at(2 * (i + 1)))
                            project(next_proj(("q", s), lo_q, i * KV + s + 1), s * P, pe_q)
                        if n in (1, 3) and in_stage(mode, s, ATT + 1):
                            attend(s, n // 2)
                        if n == V_SEG and s % 8 < 4 and mode != LAST:
                            project_v(s)
                        if n == U1_SEG and 9 <= s < 13 and mode != FIRST:
                            ffn_p(s - 9)
                        if (s, n) == Y_AT and mode != FIRST:
                            ffn_y(0)
                            ffn_y(1)
                        if (s, n) in U2_PAIRS and mode != FIRST:
                            ffn_u2(U2_PAIRS[s, n])

            iterations("pe", pe, body)

        @block.scalar
        def _(act):
            def copy(out_ap, in_ap, scale=1.0):
                return nc.scalar.activation(out_ap, in_ap, ACT.Copy, scale=scale)

            for c, stage in enumerate((qa, qb)):
                act.wait_ge(w_in[c], 16)
                src = stage[:, :, :, :].rearrange("p a b c -> p (a b c)").bitcast(F32)
                copy(wqkv[0][:, c, :], src, W_SCALE).then_inc(split_hi, 1)
            def high_x(b, pair):
                act.wait_ge(pe_ln1, at(2 * b + pair + 1))
                copy(xnt[0][:, :, pair * 256:(pair + 1) * 256],
                     t_bank[:, :].rearrange("p (c q) -> p c q", c=DC)).then_inc(hi_ln1, 1)

            high_x(0, 0)
            high_x(0, 1)

            act.wait_ge(w_in[2], 16)
            copy(wo[0][:, :, :], ot[0][:, :, :].rearrange("p a b -> p (a b)").bitcast(F32).rearrange("p (c n) -> p c n", n=D),
                 WO_SCALE).then_inc(split_hi, 1)
            act.wait_ge(w_in[3], 96)
            small = ot[1][:, :, :].rearrange("p a b -> p (a b)").bitcast(F32)
            copy(v1s[0][:, :], small[:, 0:FF], FFN_SCALE)
            copy(u2s[:, :, 0:RANK], small[:, 1024:1536].rearrange("p (c r) -> p c r", r=RANK), FFN_SCALE)
            copy(v2s[0][:, :], small[:, 1536:1536 + D], FFN_SCALE)
            copy(u1s[0][:, :, :], small[:, 1792:1792 + DC * RANK].rearrange("p (c r) -> p c r", r=RANK),
                 FFN_SCALE).then_inc(split_hi, 1)
            act.wait_ge(const_in, 64)

            def body(i, mode):
                def proj(*use):
                    return proj_bank[PROJ[use]]

                def exponentiate(s, n):
                    count = SEG * (i * KV + s - ATT) + n
                    act.wait_ge(pe_scores, at(count + 1))
                    back = 2 if s == 0 and n < 2 else 3
                    if count - back + 1 > 0:
                        act.wait_ge(lo_p, at(count - back + 1))
                    k = SEG * s + n
                    nc.scalar.activation(p_f[:, k % 3, :], score_bank[k % 2][:, :], ACT.Exp).then_inc(exp_done, 1)

                def high_p(s, n):
                    a = i * KV + s - ATT
                    act.wait_ge(exp_done, at(SEG * a + n + 1))
                    if n == 0:
                        if 2 * (a - 1) > 0:
                            act.wait_ge(pe_av, at(2 * (a - 1)))
                    k = (SEG * s + n) % (SEG * KV)
                    copy(p_hi[:, s % 2, n, :], p_f[:, k % 3, :]).then_inc(hi_p, 1)

                for s in range(KV):
                    g = i * KV + s
                    if mode == FIRST and s == ATT + 2:
                        act.wait_ge(set_done, 1)
                    for n in range(SEG):
                        if n > 0 and in_stage(mode, s, ATT):
                            high_p(s, n - 1)
                        if n == 0 and in_stage(mode, s, ATT + 1):
                            if s > 0:
                                high_p(s - 1, SEG - 1)
                            else:
                                a = i * KV - ATT - 1
                                act.wait_ge(exp_done, at(SEG * (a + 1)))
                                copy(p_hi[:, 1, SEG - 1, :], p_f[:, (SEG * KV - 1) % 3, :]).then_inc(hi_p, 1)
                        if in_stage(mode, s, ATT):
                            exponentiate(s, n)
                        if n == MAX_SEG and s % 4 == 2 and in_stage(mode, s, 6):
                            gr = i * 4 + (s - 6) // 4
                            act.wait_ge(pe_m, at(gr + 1))
                            q4 = (s - 6) // 4 - 1
                            if 32 * (2 * i + q4 // 2 + 1) > 0:
                                act.wait_ge(m_in[q4 % 2], at(32 * (2 * i + q4 // 2 + 1)))
                            copy(mt[0][:, :], proj("max", s)[0:8, :], -1.0).then_inc(hi_m, 1)
                        if n == out_segment(s) and in_stage(mode, s, ATT + 2):
                            a = g - ATT - 2
                            act.wait_ge(pe_ot, at(a + 1))
                            if s == ATT + 2:
                                if 4 * i > 0:
                                    act.wait_ge(pe_op, at(4 * i))
                            copy(ot[0][:, (s - ATT - 2) % KV, :], t_bank[:, :]).then_inc(hi_ot, 1)
                        if (s, n) in X_PAIRS and mode != LAST:
                            if X_PAIRS[s, n] == 0:
                                act.wait_ge(pe_q, at((i + 1) * KV))
                            high_x(i + 1, X_PAIRS[s, n])
                        if n == K_SEG and s % 2 == 1 and mode != LAST:
                            act.wait_ge(pe_k, at(i * (KV // 2) + (s + 1) // 2))
                            if SEG * (i * KV + s - 7) > 0:
                                act.wait_ge(pe_scores, at(SEG * (i * KV + s - 7)))
                            bank, r0 = proj("k", s), (s - 1) % RING
                            copy(kb[0:HD, r0, :], bank[0:HD, :], KV_OUT)
                            copy(kb[0:HD, r0 + 1, :], bank[HD:P, :], KV_OUT).then_inc(hi_k, 1)
                        if mode != FIRST:
                            if 9 <= s < 13 and n == LN2_SEG:
                                u = (i - 1) * 4 + s - 9
                                act.wait_ge(pe_ln2, at(u + 1 + FREE))
                                act.wait_ge(pe_pp, at(u + FREE))
                                copy(x2nt[0][:, :, :], t_bank[:, 0:D].rearrange("p (c q) -> p c q", c=DC)).then_inc(hi_ln2, 1)
                            if (s, n) in FFN_PAIRS:
                                for c in (2 * FFN_PAIRS[s, n], 2 * FFN_PAIRS[s, n] + 1):
                                    act.wait_ge(pe_h, at((i - 1) * FC + c + 1 + FREE))
                                    act.wait_ge(lo_h, at((i - 1) * FC + max(c - 1, 0) + FREE))
                                    nc.scalar.activation(h_f[:, c % 2, :], proj("h", c)[:, :], ACT.Gelu_apprx_tanh,
                                                         bias=b1c[:, c:c + 1], scale=1.0 / FFN_SCALE).then_inc(gelu_done, 1)
                            if (s, n) == QF_AT:
                                act.wait_ge(pe_u2, at(i * FC))
                                copy(qf_hi, ffn_bank[:, :], 1.0 / FFN_SCALE).then_inc(hi_qf, 1)
                        if n == q_segment(s) and mode != LAST:
                            act.wait_ge(pe_q, at(g + 1))
                            if SEG * (i * KV + s - 7) > 0:
                                act.wait_ge(pe_scores, at(SEG * (i * KV + s - 7)))
                            bank, r = proj("q", s), s % RING
                            copy(qb[0:HD, r, 0, :], bank[0:HD, :], Q_OUT)
                            copy(qb[0:HD, r, 1, :], bank[HD:P, :], Q_OUT).then_inc(hi_q, 1)
                        if n == V_SEG and s % 8 < 4 and mode != LAST:
                            t, half = s % 8, s // 8
                            act.wait_ge(pe_v, at(i * 8 + half * 4 + t + 1))
                            if 2 * (i * KV + (0 if half else -8)) > 0:
                                act.wait_ge(pe_av, at(2 * (i * KV + (0 if half else -8))))
                            copy(v_hi[:, t, half * 8:(half + 1) * 8, 0:HD],
                                 proj("v", s)[:, :].rearrange("p (k d) -> p k d", d=HD), KV_OUT).then_inc(hi_v, 1)
                        if n == U1_SEG and 9 <= s < 13 and mode != FIRST:
                            u = (i - 1) * 4 + s - 9
                            act.wait_ge(pe_pp, at(u + 1 + FREE))
                            if s == 9:
                                act.wait_ge(pe_h, at((i - 1) * FC + FREE))
                            copy(pp[0:RANK, (s - 9) * P:(s - 8) * P], proj("p", s - 9)[0:RANK, 0:P], 1.0 / FFN_SCALE).then_inc(hi_pp, 1)

            iterations("act", act, body)

        @block.vector
        def _(dve):
            def low(out_ap, bank, high, scale):
                return nc.vector.scalar_tensor_tensor(out=out_ap, in0=bank, scalar=scale, in1=high,
                                                      op0=ALU.mult, op1=ALU.subtract)

            def ln1(b):
                dve.wait_ge(x_in, at(16 * (b + 1)))
                for t in range(T):
                    last = nc.vector.bn_stats(bst[:, t, :], xt[:, t, :])
                last.then_inc(st1, 1)
                dve.wait_ge(st1, at(b + 1))
                dve.sem_inc(gate, 1)
                for t in range(T):
                    last = nc.vector.bn_aggr(agg[:, t, :], bst[:, t, :])
                last.then_inc(ag1, 1)
                dve.wait_ge(ag1, at(b + 1))
                nc.vector.tensor_scalar(veps[:, :], agg[:, :, 1], EPS, None, ALU.add).then_inc(ve1, 1)
                dve.wait_ge(rs1, at(b + 1))
                for t in range(T):
                    last = nc.vector.tensor_scalar(xt[:, t, :], xt[:, t, :], agg[:, t, 0:1], rstd[:, t:t + 1],
                                                   ALU.subtract, ALU.mult)
                last.then_inc(xn_done, 1)

            dve.sem_inc(y_done, FREE)
            dve.sem_inc(lo_qf, FREE)
            nc.vector.memset(nhalf[:, :], -0.5).then_inc(split_done, 1)
            ln1(0)
            for c, stage in enumerate((qa, qb)):
                dve.wait_ge(split_hi, at(c + 1))
                src = stage[:, :, :, :].rearrange("p a b c -> p (a b c)").bitcast(F32)
                low(wqkv[1][:, c, :], src, wqkv[0][:, c, :], W_SCALE).then_inc(split_done, 1)
            staged_wo = ot[0][:, :, :].rearrange("p a b -> p (a b)").bitcast(F32).rearrange("p (c n) -> p c n", n=D)
            small = ot[1][:, :, :].rearrange("p a b -> p (a b)").bitcast(F32)

            def split_rest(s):
                if s < 4:
                    if s == 0:
                        dve.wait_ge(split_hi, 3)
                    kv = slice(s * KV // 4, (s + 1) * KV // 4)
                    low(wo[1][:, kv, :], staged_wo[:, kv, :], wo[0][:, kv, :], WO_SCALE)
                elif s == 4:
                    dve.wait_ge(split_hi, 4)
                    low(v1s[1][:, :], small[:, 0:FF], v1s[0][:, :], FFN_SCALE)
                elif s == 5:
                    low(u2s[:, :, RANK:2 * RANK], small[:, 1024:1536].rearrange("p (c r) -> p c r", r=RANK),
                        u2s[:, :, 0:RANK], FFN_SCALE)
                    low(v2s[1][:, :], small[:, 1536:1536 + D], v2s[0][:, :], FFN_SCALE)
                    low(u1s[1][:, :, :], small[:, 1792:1792 + DC * RANK].rearrange("p (c r) -> p c r", r=RANK),
                        u1s[0][:, :, :], FFN_SCALE)
                    nc.vector.memset(v_hi[:, :, :, HD:HD + 1], 1.0).then_inc(set_done, 1)

            def low_x(b, pair):
                dve.wait_ge(hi_ln1, at(2 * b + pair + 1))
                cols = slice(pair * 256, (pair + 1) * 256)
                low(xnt[1][:, :, cols], t_bank[:, :].rearrange("p (c q) -> p c q", c=DC),
                    xnt[0][:, :, cols], 1.0).then_inc(lo_ln1, 1)

            low_x(0, 0)
            low_x(0, 1)
            dve.wait_ge(const_in, 64)

            def body(i, mode):
                def proj(*use):
                    return proj_bank[PROJ[use]]

                def maxima(s, n):
                    g = i * KV + s - 2
                    if n == 0 and (s - 2) % 4 == 0:
                        if i * 4 + (s - 2) // 4 - 1 > 0:
                            dve.wait_ge(pe_m, at(i * 4 + (s - 2) // 4 - 1))
                    dve.wait_ge(pe_max, at(SEG * g + n + 1))
                    dve.sem_inc(gate, 1)
                    for h, qt, off in MAX_BLOCKS[n]:
                        bank = max_place(s, n)[0][:, off:off + (qt + 1) * P]
                        col = 2 * ((s - 2) % 4) + h
                        last = nc.vector.tensor_tensor_reduce(
                            out=bank, in0=bank, in1=causal[:, (T - 1 - qt) * P:S], scale=1.0, scalar=-3e38,
                            op0=ALU.add, op1=ALU.max, accum_out=mcol[:, (s - 2) // 4 % 2, qt, col:col + 1])
                    last.then_inc(max_done, 1)

                def normalise(s, h):
                    a = i * KV + s - ATT - 1
                    dve.wait_ge(pe_av, at(2 * a + h + 1))
                    o = o_bank[:, 0:T * (HD + 1)].rearrange("p (t c) -> p t c", t=T)
                    nc.vector.reciprocal(rden[:, h, :], o[:, :, HD]).then_inc(recip_done, 1)
                    if h == 0:
                        if a > 0:
                            dve.wait_ge(pe_ot, at(a))
                    dve.wait_ge(recip_done, at(2 * a + h + 1))
                    nc.vector.tensor_tensor(o_f[:, :, h * HD:(h + 1) * HD], o[:, :, 0:HD],
                                            rden[:, h, :].unsqueeze(2).to_broadcast([P, T, HD]),
                                            ALU.mult).then_inc(o_done, 1)

                for s in range(KV):
                    g = i * KV + s
                    for n in range(SEG):
                        if n == 0 and 9 <= s < 13 and mode != FIRST:
                            t = s - 9
                            u = (i - 1) * 4 + t
                            dve.wait_ge(rs2, at(u + 1))
                            if t == 0:
                                dve.wait_ge(lo_h, at((i - 1) * FC + FREE))
                            dve.wait_ge(pe_ln2, at(u + FREE))
                            nc.vector.tensor_scalar(x2n[:, :], x2[:, t, :], agg2[:, t, 0:1], rstd2[:, t:t + 1],
                                                    ALU.subtract, ALU.mult).then_inc(x2n_done, 1)
                        if n == MAX_SEG and s % 4 == 2 and in_stage(mode, s, 6):
                            dve.wait_ge(hi_m, at(i * 4 + (s - 6) // 4 + 1))
                            low(mt[1][:, :], proj("max", s)[0:8, :], mt[0][:, :], -1.0).then_inc(lo_m, 1)
                        if in_stage(mode, s, 2):
                            maxima(s, n)
                        sv, segment = before(s, n, v_lag(s))
                        if segment == V_SEG and sv % 8 < 4 and mode != LAST:
                            t, half = sv % 8, sv // 8
                            heads = slice(half * 8, (half + 1) * 8)
                            dve.wait_ge(hi_v, at(i * 8 + half * 4 + t + 1))
                            low(v_lo[:, t, heads, :], proj("v", sv)[:, :].rearrange("p (k d) -> p k d", d=HD),
                                v_hi[:, t, heads, 0:HD], KV_OUT).then_inc(lo_v, 1)
                        if n == out_segment(s) + out_lag(s) and in_stage(mode, s, ATT + 2):
                            dve.wait_ge(hi_ot, at(g - ATT - 1))
                            low(ot[1][:, (s - ATT - 2) % KV, :], t_bank[:, :], ot[0][:, (s - ATT - 2) % KV, :],
                                1.0).then_inc(lo_ot, 1)
                        if (s, n) in X_PAIRS and mode != LAST:
                            low_x(i + 1, X_PAIRS[s, n])
                        if n == K_SEG + k_lag(s) and s % 2 == 1 and mode != LAST:
                            dve.wait_ge(hi_k, at(i * (KV // 2) + (s + 1) // 2))
                            bank, r0 = proj("k", s), (s - 1) % RING
                            low(ka[0:HD, r0, :], bank[0:HD, :], kb[0:HD, r0, :], KV_OUT)
                            low(ka[0:HD, r0 + 1, :], bank[HD:P, :], kb[0:HD, r0 + 1, :], KV_OUT).then_inc(lo_k, 1)
                        if n == q_segment(s) + q_lag(s) and mode != LAST:
                            dve.wait_ge(hi_q, at(g + 1))
                            bank, r = proj("q", s), s % RING
                            low(qa[HD:P, r, 0, :], bank[0:HD, :], qb[0:HD, r, 0, :], Q_OUT)
                            low(qa[HD:P, r, 1, :], bank[HD:P, :], qb[0:HD, r, 1, :], Q_OUT).then_inc(lo_q, 1)
                        if mode != FIRST:
                            if s == 8 and n >= 1:
                                t = n - 1
                                u = (i - 1) * 4 + t
                                if t == 0:
                                    dve.wait_ge(x2_in, at(16 * i))
                                dve.wait_ge(pe_op, at(u + 1))
                                nc.vector.scalar_tensor_tensor(out=x2[:, t, :], in0=proj("out", t)[:, 0:D], scalar=1.0 / WO_SCALE,
                                                               in1=x2[:, t, :], op0=ALU.mult, op1=ALU.add).then_inc(x2_done, 1)
                                dve.wait_ge(x2_done, at(u + 1))
                                nc.vector.bn_stats(bst2[:, t, :], x2[:, t, :]).then_inc(st2, 1)
                                dve.wait_ge(st2, at(u + 1))
                                dve.sem_inc(gate, 1)
                                nc.vector.bn_aggr(agg2[:, t, :], bst2[:, t, :]).then_inc(ag2, 1)
                                dve.wait_ge(ag2, at(u + 1))
                                nc.vector.tensor_scalar(veps2[:, t:t + 1], agg2[:, t, 1:2], EPS, None, ALU.add).then_inc(ve2, 1)
                            if 9 <= s < 13 and n == LN2_SEG:
                                u = (i - 1) * 4 + s - 9
                                dve.wait_ge(hi_ln2, at(u + 1))
                                low(x2nt[1][:, :, :], t_bank[:, 0:D].rearrange("p (c q) -> p c q", c=DC),
                                    x2nt[0][:, :, :], 1.0).then_inc(lo_ln2, 1)
                            if (s, n) in FFN_PAIRS:
                                pair = FFN_PAIRS[s, n]
                                for c in (2 * pair, 2 * pair + 1):
                                    dve.wait_ge(gelu_done, at((i - 1) * FC + c + 1))
                                    if c >= 2:
                                        dve.wait_ge(pe_u2, at((i - 1) * FC + c - 1))
                                    elif c == 0:
                                        dve.wait_ge(pe_y, at(2 * (i - 1) + FREE))
                                    nc.vector.tensor_copy(h_hi[:, c % 2, :], h_f[:, c % 2, :]).then_inc(hi_h, 1)
                            if (s, n) == QF_AT:
                                dve.wait_ge(hi_qf, at(i))
                                low(qf_lo, ffn_bank[:, :], qf_hi, 1.0 / FFN_SCALE).then_inc(lo_qf, 1)
                            if (s, n) == Y_AT:
                                for pair in range(2):
                                    dve.wait_ge(pe_y, at(2 * (i - 1) + pair + 1 + FREE))
                                    if pair == 0:
                                        dve.wait_ge(b2_done, at(4 * i))
                                    rows = x2[:, 2 * pair:2 * pair + 2, :]
                                    nc.vector.scalar_tensor_tensor(out=rows, in0=proj("y", pair)[:, :].rearrange("p (t d) -> p t d", d=D),
                                                                   scalar=1.0 / FFN_SCALE, in1=rows, op0=ALU.mult,
                                                                   op1=ALU.add).then_inc(y_done, 1)
                        if n in (1, 3) and in_stage(mode, s, ATT + 1):
                            normalise(s, n // 2)
                        if n == U1_SEG and 9 <= s < 13 and mode != FIRST:
                            dve.wait_ge(hi_pp, at((i - 1) * 4 + s - 8))
                            cols = slice((s - 9) * P, (s - 8) * P)
                            low(pp[RANK:P, cols], proj("p", s - 9)[0:RANK, 0:P], pp[0:RANK, cols], 1.0 / FFN_SCALE).then_inc(lo_pp, 1)
                    if s == 7 and mode != LAST:
                        ln1(i + 1)
                    if mode == FIRST:
                        split_rest(s)

            iterations("dve", dve, body)

        @block.gpsimd
        def _(pool):
            pool.sem_inc(lo_h, FREE)
            pool.wait_ge(split_done, 1)

            def power1(b):
                pool.wait_ge(ve1, at(b + 1))
                nc.gpsimd.tensor_tensor(rstd[:, :], veps[:, :], nhalf[:, :], ALU.pow).then_inc(rs1, 1)

            power1(0)
            pool.wait_ge(rs1, 1)
            nc.gpsimd.memset(kb[HD:P, :, :].bitcast(F32), 0.0).then_inc(k_rows, 1)
            pool.wait_ge(k_rows, 1)
            nc.gpsimd.memset(kb[MAX0:MAX0 + 2, :, :], 1.0).then_inc(k_rows, 1)
            pool.wait_ge(k_rows, 2)
            pool.wait_ge(split_done, 3)
            nc.gpsimd.memset(qb[HD:P, :, :, :].bitcast(F32), 0.0).then_inc(zeroed, 1)
            pool.wait_ge(zeroed, 1)

            def body(i, mode):
                def low_p(count, slot, n, k):
                    pool.wait_ge(hi_p, at(count + 1))
                    nc.gpsimd.tensor_tensor(p_lo[:, slot, n, :], p_f[:, k % 3, :], p_hi[:, slot, n, :],
                                            ALU.subtract).then_inc(lo_p, 1)

                for s in range(KV):
                    for n in range(SEG):
                        if n > 0 and in_stage(mode, s, ATT):
                            low_p(SEG * (i * KV + s - ATT) + n - 1, s % 2, n - 1, SEG * s + n - 1)
                        if n == 0 and in_stage(mode, s, ATT + 1):
                            low_p(SEG * (i * KV + s - ATT) - 1, (s - 1) % 2, SEG - 1, (SEG * s - 1) % (SEG * KV))
                        if mode != FIRST:
                            if s == 8 and n >= 1:
                                t = n - 1
                                pool.wait_ge(ve2, at((i - 1) * 4 + t + 1))
                                nc.gpsimd.tensor_tensor(rstd2[:, t:t + 1], veps2[:, t:t + 1], nhalf[:, 0:1],
                                                        ALU.pow).then_inc(rs2, 1)
                            if 9 <= s < 13 and n == 1:
                                t = s - 9
                                pool.wait_ge(x2n_done, at((i - 1) * 4 + t + 1))
                                nc.gpsimd.tensor_tensor(x2[:, t, :], x2[:, t, :], b2b[:, :], ALU.add).then_inc(b2_done, 1)
                            if (s, n) in FFN_PAIRS:
                                pair = FFN_PAIRS[s, n]
                                for c in (2 * pair, 2 * pair + 1):
                                    pool.wait_ge(hi_h, at((i - 1) * FC + c + 1))
                                    nc.gpsimd.tensor_tensor(h_lo[:, c % 2, :], h_f[:, c % 2, :], h_hi[:, c % 2, :],
                                                            ALU.subtract).then_inc(lo_h, 1)
                    if s == 7 and mode != LAST:
                        power1(i + 1)

            pool.wait_ge(const_in, 64)
            iterations("pool", pool, body)


_NAMES = ["L0_attn_inputs", "L0_attn_W_qkv", "L0_attn_W_out", "L0_ffn_U1", "L0_ffn_V1", "L0_ffn_b1",
          "L0_ffn_U2", "L0_ffn_V2", "L0_ffn_b2"]


def constants():
    import numpy as np

    slope = (np.float64(2.0) ** -0.25) ** np.arange(1, 2 * KV + 1)
    slope = slope.astype(np.float32).astype(np.float64)
    s1 = slope.astype(np.float16).astype(np.float64)
    s2 = (slope - s1).astype(np.float16).astype(np.float64)
    pos = np.arange(S, dtype=np.float64)
    sk = (s1 + s2)[:, None] * pos[None, :]
    parts = []
    for _ in range(3):
        part = sk.astype(np.float16).astype(np.float64)
        parts.append(part)
        sk = sk - part
    k_aug = np.zeros((AUG, KV, S), np.float16)
    q_aug = np.zeros((AUG, RING, 2, S), np.float16)
    for h in range(2):
        rows = [parts[0][h::2], np.broadcast_to(-s1[h::2, None], (KV, S)), parts[1][h::2],
                np.broadcast_to(-s2[h::2, None], (KV, S)), parts[2][h::2]]
        for j, row in enumerate(rows):
            k_aug[5 * h + j] = row.astype(np.float16)
            q_aug[5 * h + j, :, h, :] = (pos if j in (1, 3) else np.ones(S)).astype(np.float16)
    ident = np.eye(P, dtype=np.float32)
    causal = np.zeros((P, S), np.float32)
    causal[:, S - P:] = np.where(np.arange(P)[None, :] > np.arange(P)[:, None], np.float32(-1e30), np.float32(0))
    return k_aug, q_aug.reshape(AUG, RING * 2 * S), ident, causal


def kernel(**inputs):
    import ml_dtypes
    import numpy as _np
    import concourse.bacc as _bacc
    from concourse import mybir as _mybir
    from concourse.bass_utils import run_bass_kernel_spmd as _run

    nc = _bacc.Bacc("TRN2", target_bir_lowering=False, num_devices=1)
    arrays, args = {}, []
    k_aug, q_aug, ident, causal = constants()
    consts = {"k_aug": k_aug, "q_aug": q_aug, "ident": ident, "ident_b": ident.astype(ml_dtypes.bfloat16), "causal": causal.astype(ml_dtypes.bfloat16)}
    for name, a in [(n, inputs[n]) for n in _NAMES] + list(consts.items()):
        if name == "L0_ffn_b1":
            a = _np.asarray(a).reshape(FC, P).T
        a = _np.ascontiguousarray(a)
        arrays[f"in_{name}"] = a
        args.append(nc.dram_tensor(f"in_{name}", a.shape, _mybir.dt.from_np(a.dtype), kind="ExternalInput").ap())
    out = nc.dram_tensor("out_0", inputs["L0_attn_inputs"].shape, F32, kind="ExternalOutput").ap()
    layer(nc, *args, out)
    r = _run(nc, [arrays], core_ids=[0])
    return r.results[0]["out_0"]
```
